# Optimizing a Trainium2 kernel written in Bass

```python
import numpy as np
import jax
import jax.numpy as jnp

def _softmax(x, axis=-1):
    return jax.nn.softmax(x, axis=axis)

def _gelu(x):
    return jax.nn.gelu(x, approximate=True)

def _silu(x):
    return jax.nn.silu(x)

def _sigmoid(x):
    return jax.nn.sigmoid(x)

def _layernorm(x, axis=-1, eps=1e-05):
    m = jnp.mean(x, axis=axis, keepdims=True)
    v = jnp.var(x, axis=axis, keepdims=True)
    return (x - m) / jnp.sqrt(v + eps)

def _scatter_add(tgt, idx, src, axis=0):
    return tgt.at[idx].add(src)

def _segment_sum(src, seg, n):
    return jax.ops.segment_sum(src, seg, n)
kernel_name = 'mk_gnn_preln_d1_gnn_r64_968ece'

def setup_inputs(seed: int=0):
    np.random.seed(seed)
    _w = jnp.asarray

    def _rec_inputs():
        import jax
        import jax.numpy as jnp
        _gk = jax.random.key(seed)
        x = -8.776e-05 + 1 * jax.random.normal(jax.random.fold_in(_gk, 1), (50000, 512), jnp.float32)
        src = jax.random.randint(jax.random.fold_in(_gk, 2), (12500,), 0, 50000, jnp.int32)
        dst = jax.random.randint(jax.random.fold_in(_gk, 3), (12500,), 0, 50000, jnp.int32)
        _o = jnp.argsort(dst, stable=True)
        src = src[_o]
        dst = dst[_o]
        return (x, src, dst)
    x, src, dst = _rec_inputs()

    def _L0_gnn_setup():
        import jax, jax.numpy as jnp
        import numpy as np
        N_NODES = 10000
        IN_FEAT = 512
        OUT_FEAT = 512
        N_EDGES = 2500
        key = jax.random.key(seed)
        kx, kw, ks, kd = jax.random.split(key, 4)
        x = jax.random.normal(kx, (N_NODES, IN_FEAT), dtype=jnp.float32)
        fan_in, fan_out = (2 * IN_FEAT, OUT_FEAT)
        limit = float(np.sqrt(6.0 / (fan_in + fan_out)))
        w = jax.random.uniform(kw, (OUT_FEAT, 2 * IN_FEAT), dtype=jnp.float32, minval=-limit, maxval=limit)
        src = jax.random.randint(ks, (N_EDGES,), 0, N_NODES, dtype=jnp.int32)
        dst = jax.random.randint(kd, (N_EDGES,), 0, N_NODES, dtype=jnp.int32)
        edge_index = jnp.stack([src, dst], axis=0)
        return {'x': x, 'w': w, 'edge_index': edge_index}
    _L0_gnn_all = _L0_gnn_setup()
    _L0_gnn_in = {k: v for k, v in _L0_gnn_all.items() if k in ('w',)}
    del _L0_gnn_all
    return {'x': x, 'src': src, 'dst': dst, 'L0_gnn_w': _L0_gnn_in['w']}

def reference(x, src, dst, L0_gnn_w):
    import jax
    import jax.numpy as jnp

    def _L0_gnn_ref(x, w, edge_index):
        import jax, jax.numpy as jnp
        import numpy as np
        N_NODES = 10000
        IN_FEAT = 512
        OUT_FEAT = 512
        N_EDGES = 2500
        src, dst = (edge_index[0], edge_index[1])
        msgs = x[src]
        summed = jax.ops.segment_sum(msgs, dst, num_segments=x.shape[0])
        deg = jax.ops.segment_sum(jnp.ones_like(dst, dtype=x.dtype), dst, num_segments=x.shape[0])
        neighbor_mean = summed / jnp.maximum(deg, 1.0)[:, None]
        message = jnp.concatenate([x, neighbor_mean], axis=-1)
        weighted = jnp.einsum('of,nf->no', w, message)
        return jax.nn.relu(weighted)
    edge_index = jnp.stack([src, dst])
    h = jnp.maximum(_layernorm(x, axis=-1), 0.0)
    x = x + _L0_gnn_ref(h, L0_gnn_w, edge_index)
    return x

_drawn_inputs = setup_inputs


def setup_inputs(seed=0):
    import zlib

    import numpy as np

    out = dict(_drawn_inputs(seed))
    spreads = {}
    factors = {}
    for name, (base, spread) in spreads.items():
        noise = np.random.default_rng([zlib.crc32(name.encode()), seed]).standard_normal(out[name].shape)
        drawn = base * np.exp(spread * noise) if base else spread * noise
        out[name] = jnp.asarray(drawn.astype(out[name].dtype))
    for name, factor in factors.items():
        out[name] = (out[name] * factor).astype(out[name].dtype)
    return out
```

```python
from contextlib import ExitStack

import concourse.bass as bass
from concourse import mybir

F32 = mybir.dt.float32
F32R = mybir.dt.float32r
I32 = mybir.dt.int32
ALU = mybir.AluOpType
ACT = mybir.ActivationFunctionType
AX = mybir.AxisListType

P = 128
EPS = 1e-5


def build(nc, x, src, dst, w, out):
    N, F = x.shape
    E = src.shape[0]
    O = w.shape[0]
    FC = F // P
    OC = O // P
    KW = 2 * FC

    TN = N // P
    NTAIL = N - TN * P
    U = 3
    XR = 6
    NB = U * XR
    NT = TN + 1
    TE = -(-E // P)
    EFULL = E // P
    ETAIL = E - EFULL * P
    EP = TE * P
    EB = 6
    PAD = 1 << 16
    NOWHERE = 1 << 20
    assert TN % U == 0 and E // TE == P - 1 and E % TE and N < PAD and EP < NOWHERE and 0 < NTAIL and 0 < ETAIL

    a_dram = nc.dram_tensor("edge_rows", [EP, O], F32, kind="Internal").ap()
    slot_dram = nc.dram_tensor("slot_of_node", [N, 1], I32, kind="Internal").ap()
    sdst_dram = nc.dram_tensor("sorted_dst", [EP, 1], I32, kind="Internal").ap()
    ssrc_dram = nc.dram_tensor("sorted_src", [EP, 1], I32, kind="Internal").ap()

    x_grid = x[0:TN * P, :].rearrange("(p t) f -> p t f", t=TN)
    out_grid = out[0:TN * P, :].rearrange("(p t) f -> p t f", t=TN)
    a_tiles = a_dram.rearrange("(j p) o -> p j o", p=P)

    ctx = ExitStack()
    with ctx:
        def sb(name, shape, dt=F32):
            return ctx.enter_context(nc.sbuf_tensor(name, shape, dt))

        def pb(name):
            return ctx.enter_context(nc.psum_tensor(name, [P, 512], F32))

        def sem(name):
            return ctx.enter_context(nc.semaphore(name))

        ident = sb("ident", [P, P])
        ones = sb("ones", [P, P])
        eps = sb("eps", [P, 1])
        w_rows = sb("w_rows", [P, OC, 2 * F])
        w_hi = sb("w_hi", [P, KW, O], F32R)
        w_lo = sb("w_lo", [P, KW, O], F32R)

        d_row = sb("d_row", [TE, P], I32)
        d_next = sb("d_next", [TE, P], I32)
        d_prev = sb("d_prev", [TE, P], I32)
        s_row = sb("s_row", [TE, P], I32)
        e_row = sb("e_row", [TE, P], I32)
        d_all = sb("d_all", [P, EP], I32)
        descent = sb("descent", [TE, P])
        descents = sb("descents", [TE, 1])
        unsorted_flag = sb("unsorted_flag", [1, 1], I32)
        begins = sb("begins", [TE, P])
        run_begin = sb("run_begin", [TE, P])
        begin_row = sb("begin_row", [1, TE + 1])
        rdeg_row = sb("rdeg_row", [TE, P])
        not_last = sb("not_last", [TE, P])
        scatter_row = sb("scatter_row", [TE, P])
        sf_row = sb("sf_row", [TE, P])
        df_row = sb("df_row", [TE, P])
        d_col = sb("d_col", [P, TE])
        rdeg_col = sb("rdeg_col", [P, TE])
        edge_cols = sb("edge_cols", [P, TE, 3], I32)
        none_yet = sb("none_yet", [P, TN + 1], I32)
        slots = sb("slots", [P, NT], I32)
        has_edges = sb("has_edges", [P, NT])

        xe = sb("xe", [P, EB, F])
        edge_idx = sb("edge_idx", [P, EB, 3], I32)
        e_bn = sb("e_bn", [P, 3, 2, 6])
        e_mv = sb("e_mv", [P, 3, 2, 2])
        e_small = sb("e_small", [P, 3, 6, 2])
        he = sb("he", [P, 3, F])
        same = sb("same", [P, 2, P])
        goes_on = sb("goes_on", [P, 2, P])
        agg = sb("agg", [P, 3, FC, P])
        op_hi = sb("op_hi", [P, 3, FC, P], F32R)
        op_lo = sb("op_lo", [P, 3, FC, P], F32R)
        agg_hi, agg_lo, h_hi, h_lo = op_hi, op_lo, op_hi, op_lo
        a_out = sb("a_out", [P, 3, O])

        xn = sb("xn", [P, XR, U, F])
        n_bn = sb("n_bn", [P, 3, U, 6])
        n_mv = sb("n_mv", [P, 3, U, 2])
        n_small = sb("n_small", [P, 3, 6, U])
        hn = sb("hn", [P, 3, F])
        gathered = xe
        node_idx = sb("node_idx", [P, 3, U], I32)
        y = a_out

        NC = 16
        CH = EP // NC
        xe_flat = xe[:, :, :].rearrange("p k f -> p (k f)")
        chunk_pos, earlier, tied = (xe_flat[:, n * CH:(n + 1) * CH] for n in range(3))
        u_dst = sb("u_dst", [P, TE], I32)
        u_src = sb("u_src", [P, TE], I32)
        u_dstf = sb("u_dstf", [P, TE])
        e_col = sb("e_col", [P, TE])
        counts = sb("counts", [P, 2 * NC])
        count = sb("count", [P, 1])
        rank = sb("rank", [P, TE], I32)
        sort_cols = sb("sort_cols", [P, 4], I32)

        ps_sum = [pb("ps_sum0"), pb("ps_sum1")]
        ps_a = [pb("ps_a0"), pb("ps_a1")]
        ps_t = [pb("ps_t0"), pb("ps_t1")]
        ps_y = [pb("ps_y0"), pb("ps_y1")]
        ps_w = [ps_t[0], ps_t[1], ps_y[0], ps_y[1]]

        w_loaded = sem("w_loaded")
        pads_set = sem("pads_set")
        edges_loaded = sem("edges_loaded")
        all_loaded = sem("all_loaded")
        ident_zero = sem("ident_zero")
        ident_set = sem("ident_set")
        consts_set = sem("consts_set")
        w_turned = sem("w_turned")
        w_hi_set = sem("w_hi_set")
        w_lo_set = sem("w_lo_set")
        descents_set = sem("descents_set")
        flag_summed = sem("flag_summed")
        flag_set = sem("flag_set")
        edges_sorted = sem("edges_sorted")
        none_set = sem("none_set")
        slots_cleared = sem("slots_cleared")
        setup_step = sem("setup_step")
        runs_set = sem("runs_set")
        ends_turned = sem("ends_turned")
        carry_row_set = sem("carry_row_set")
        carry_turned = sem("carry_turned")
        rows_set = sem("rows_set")
        rows_turned = sem("rows_turned")
        cols_set = sem("cols_set")
        slots_loaded = sem("slots_loaded")
        mask_set = sem("mask_set")
        sort_loaded = sem("sort_loaded")
        sort_step = sem("sort_step")
        ranks_set = sem("ranks_set")
        sort_copied = sem("sort_copied")
        sort_moved = sem("sort_moved")
        e_idx_set = sem("e_idx_set")
        e_gathered = [sem(f"e_gathered{k}") for k in range(EB)]
        e_slotted = [sem(f"e_slotted{k}") for k in range(EB)]
        e_stats = sem("e_stats")
        e_aggr = sem("e_aggr")
        e_sd = sem("e_sd")
        e_chain = sem("e_chain")
        e_h = sem("e_h")
        e_same = sem("e_same")
        e_summed = sem("e_summed")
        e_agg = sem("e_agg")
        e_hi = sem("e_hi")
        e_lo = sem("e_lo")
        e_product = sem("e_product")
        e_out = sem("e_out")
        e_stored = [sem(f"e_stored{k}") for k in range(3)]
        n_loaded = [sem(f"n_loaded{k}") for k in range(XR)]
        n_stored = [sem(f"n_stored{k}") for k in range(XR)]
        n_idx_set = sem("n_idx_set")
        n_gathered = [sem(f"n_gathered{k}") for k in range(6)]
        n_stats = sem("n_stats")
        n_aggr = sem("n_aggr")
        n_sd = sem("n_sd")
        n_chain = sem("n_chain")
        n_h = sem("n_h")
        n_turned = sem("n_turned")
        n_hi = sem("n_hi")
        n_lo = sem("n_lo")
        n_product = sem("n_product")
        n_y = sem("n_y")
        n_relu = sem("n_relu")
        n_added = sem("n_added")

        CHAIN = 6

        def loop(eng, tiles, body, step, ahead=0):
            full = (tiles - ahead) // body
            for k in range(body):
                step(0, k)
            with eng.Fori(1, full) as it:
                for k in range(body):
                    step(it, k)
            for k in range(tiles - full * body):
                step(full + k // body, k % body)

        def later(i, body, by):
            it, k = i
            return it + (k + by) // body, (k + by) % body

        def is_first(it):
            return isinstance(it, int) and it == 0

        NLAST = NT // NB
        ELAST = TE // EB

        def n_inside(it, k):
            return not isinstance(it, int) or it * NB + k < NT

        def e_inside(it, k):
            return not isinstance(it, int) or it * EB + k < TE

        def n_rows(it, k):
            return NTAIL if isinstance(it, int) and it * NB + k == TN else P

        block = ctx.enter_context(nc.Block())

        @block.sync
        def _(sp):
            sp.wait_ge(pads_set, 5)
            sp.dma_start(d_row[0:EFULL, :], dst[0:EFULL * P].rearrange("(j i) -> j i", i=P)).then_inc(edges_loaded, 16)
            sp.dma_start(d_row[EFULL:TE, 0:ETAIL], dst[EFULL * P:E].rearrange("(j i) -> j i", j=1)).then_inc(edges_loaded, 16)
            sp.dma_start(d_next[0:EFULL, :], dst[1:EFULL * P + 1].rearrange("(j i) -> j i", i=P)).then_inc(edges_loaded, 16)
            sp.dma_start(d_next[EFULL:TE, 0:ETAIL - 1], dst[EFULL * P + 1:E].rearrange("(j i) -> j i", j=1)).then_inc(edges_loaded, 16)
            sp.dma_start(w_rows[:, :, :], w.rearrange("(b p) f -> p b f", p=P)).then_inc(w_loaded, 16)
            sp.dma_start(d_prev[0:1, 1:P], dst[0:P - 1].rearrange("(j i) -> j i", j=1)).then_inc(edges_loaded, 16)
            sp.dma_start(d_prev[1:EFULL, :], dst[P - 1:EFULL * P - 1].rearrange("(j i) -> j i", i=P)).then_inc(edges_loaded, 16)
            sp.dma_start(d_prev[EFULL:TE, 0:ETAIL + 1], dst[EFULL * P - 1:E].rearrange("(j i) -> j i", j=1)).then_inc(edges_loaded, 16)
            sp.dma_start(s_row[0:EFULL, :], src[0:EFULL * P].rearrange("(j i) -> j i", i=P)).then_inc(edges_loaded, 16)
            sp.dma_start(s_row[EFULL:TE, 0:ETAIL], src[EFULL * P:E].rearrange("(j i) -> j i", j=1)).then_inc(edges_loaded, 16)
            sp.dma_start(d_all[:, 0:E], dst.partition_broadcast(P)).then_inc(all_loaded, 16)

            def load_group(it, s):
                t0 = it * NB + s * U
                if isinstance(it, int) and t0 >= TN:
                    if t0 == TN:
                        sp.dma_start(xn[0:NTAIL, s, 0, :], x[TN * P:N, :]).then_inc(n_loaded[s], 16)
                    return
                sp.dma_start(xn[:, s, :, :], x_grid[:, bass.ds(t0, U), :]).then_inc(n_loaded[s], 16)

            for s in range(XR - 1):
                load_group(0, s)

            def store_edges(it, k):
                sp.wait_ge(e_out, it * EB + k + 1)
                sp.dma_start(a_tiles[:, bass.ds(it * EB + k, 1), :],
                             a_out[:, k % 3:k % 3 + 1, :]).then_inc(e_stored[k % 3], 16)

            loop(sp, TE, EB, store_edges)

            def node_group(it, s):
                b, ks = later((it, s), XR, XR - 1)
                if not (is_first(it) and s == 0):
                    pit, pk = later((it, s), XR, -1)
                    sp.wait_ge(n_stored[pk], 16 * (pit + 1))
                load_group(b, ks)
                t0 = it * NB + s * U
                if isinstance(it, int) and t0 >= TN:
                    sp.wait_ge(n_added, TN + 1)
                    sp.dma_start(out[TN * P:N, :], xn[0:NTAIL, s, 0, :]).then_inc(n_stored[s], 16)
                    return
                sp.wait_ge(n_added, t0 + U)
                sp.dma_start(out_grid[:, bass.ds(t0, U), :], xn[:, s, :, :]).then_inc(n_stored[s], 16)

            groups = TN // U + 1
            loop(sp, groups, XR, node_group, XR)
            for s in range(XR):
                sp.wait_ge(n_stored[s], 16 * len(range(s, groups, XR)))

        @block.gpsimd
        def _(pool):
            nc.gpsimd.memset(d_row[:, :], PAD).then_inc(pads_set, 1)
            nc.gpsimd.memset(d_next[:, :], PAD).then_inc(pads_set, 1)
            nc.gpsimd.memset(d_prev[:, :], PAD).then_inc(pads_set, 1)
            nc.gpsimd.memset(s_row[:, :], 0).then_inc(pads_set, 1)
            nc.gpsimd.memset(d_all[:, E:EP], PAD).then_inc(pads_set, 1)
            nc.gpsimd.memset(ident[:, :], 0.0).then_inc(ident_zero, 1)
            nc.gpsimd.memset(ones[:, :], 1.0).then_inc(consts_set, 1)
            pool.wait_ge(ident_zero, 1)
            nc.gpsimd.affine_select(out=ident[:, :], in_=ident[:, :], compare_op=ALU.not_equal, fill=1.0,
                                    base=0, pattern=[[-1, P]], channel_multiplier=1).then_inc(ident_set, 1)
            nc.gpsimd.memset(eps[:, :], EPS).then_inc(consts_set, 1)
            nc.gpsimd.iota(e_row[:, :], pattern=[[1, P]], base=0, channel_multiplier=P).then_inc(consts_set, 1)
            nc.gpsimd.iota(edge_cols[:, :, 2], pattern=[[P, TE]], base=0, channel_multiplier=1).then_inc(consts_set, 1)
            nc.gpsimd.memset(none_yet[:, :], NOWHERE).then_inc(none_set, 1)
            pool.wait_ge(none_set, 1)
            pool.dma_start(slot_dram[0:TN * P, :].rearrange("(p t) a -> p (t a)", t=TN),
                           none_yet[:, 0:TN]).then_inc(slots_cleared, 16)
            pool.dma_start(slot_dram[TN * P:N, :], none_yet[0:NTAIL, 0:1]).then_inc(slots_cleared, 16)

            pool.wait_ge(flag_set, 1)
            pool.wait_ge(edges_loaded, 16 * 9)
            pool.wait_ge(all_loaded, 16)
            flag = pool.value_load(unsorted_flag[0:1, 0:1], min_val=0, max_val=EP)
            with pool.If(flag > 0):
                nc.gpsimd.memset(u_dst[:, :], PAD).then_inc(sort_copied, 1)
                nc.gpsimd.memset(u_src[:, :], 0).then_inc(sort_copied, 1)
                pool.wait_ge(sort_copied, 2)
                PF = E // TE
                for to, of in ((u_dst, dst), (u_src, src)):
                    pool.dma_start(to[0:PF, :], of[0:PF * TE].rearrange("(p j) -> p j", j=TE)).then_inc(sort_loaded, 16)
                    pool.dma_start(to[PF:PF + 1, 0:E - PF * TE], of[PF * TE:E].rearrange("(p j) -> p j", p=1)).then_inc(sort_loaded, 16)
                nc.gpsimd.iota(chunk_pos, pattern=[[1, CH]], base=0, channel_multiplier=0,
                               allow_small_or_imprecise_dtypes=True).then_inc(sort_copied, 1)
                nc.gpsimd.iota(e_col[:, :], pattern=[[1, TE]], base=0, channel_multiplier=TE,
                               allow_small_or_imprecise_dtypes=True).then_inc(sort_copied, 1)
                pool.wait_ge(ranks_set, TE)
                with pool.Fori(0, TE) as j:
                    nc.gpsimd.tensor_copy(sort_cols[:, 0:1], rank[:, bass.ds(j, 1)]).then_inc(sort_copied, 1)
                    nc.gpsimd.tensor_copy(sort_cols[:, 1:2], u_dst[:, bass.ds(j, 1)]).then_inc(sort_copied, 1)
                    nc.gpsimd.tensor_copy(sort_cols[:, 2:3], u_src[:, bass.ds(j, 1)]).then_inc(sort_copied, 1)
                    pool.wait_ge(sort_copied, j * 3 + 7)
                    nc.gpsimd.tensor_tensor(sort_cols[:, 3:4], sort_cols[:, 1:2], sort_cols[:, 2:3], ALU.add)
                    pool.indirect_dma_start(sdst_dram, bass.IndirectOffsetOnAxis(sort_cols[:, 0:1], 0),
                                            sort_cols[:, 1:2], None, bounds_check=EP - 1,
                                            oob_is_err=False).then_inc(sort_moved, 16)
                    pool.indirect_dma_start(ssrc_dram, bass.IndirectOffsetOnAxis(sort_cols[:, 0:1], 0),
                                            sort_cols[:, 2:3], None, bounds_check=EP - 1,
                                            oob_is_err=False).then_inc(sort_moved, 16)
                    pool.wait_ge(sort_moved, j * 32 + 32)
                sd = sdst_dram.rearrange("e a -> (e a)")
                ss = ssrc_dram.rearrange("e a -> (e a)")
                loads = [
                    (d_row[:, :], sd.rearrange("(j i) -> j i", i=P)),
                    (s_row[:, :], ss.rearrange("(j i) -> j i", i=P)),
                    (d_next[0:TE - 1, :], sd[1:EP - P + 1].rearrange("(j i) -> j i", i=P)),
                    (d_next[TE - 1:TE, 0:P - 1], sd[EP - P + 1:EP].rearrange("(j i) -> j i", j=1)),
                    (d_prev[0:1, 1:P], sd[0:P - 1].rearrange("(j i) -> j i", j=1)),
                    (d_prev[1:TE, :], sd[P - 1:EP - 1].rearrange("(j i) -> j i", i=P)),
                    (d_all[:, :], sd.partition_broadcast(P)),
                ]
                for to, of in loads:
                    pool.dma_start(to, of).then_inc(sort_loaded, 16)
                pool.wait_ge(sort_loaded, 16 * (4 + len(loads)))
            nc.gpsimd.memset(sort_cols[:, :], 0).then_inc(edges_sorted, 1)

            pool.wait_ge(cols_set, 4)

            def copy_edge_cols(it, k):
                if not e_inside(it, k):
                    return
                early = is_first(it) and k < EB
                it, k = later((it, k), EB, 0)
                if not early:
                    pool.wait_ge(e_slotted[k], it * 16)
                    pool.wait_ge(e_gathered[k], it * 16)
                if not (early and k == 0):
                    pool.wait_ge(e_idx_set, it * EB + k)
                nc.gpsimd.tensor_copy(edge_idx[:, k, :].rearrange("p (a c) -> p a c", a=1),
                                      edge_cols[:, bass.ds(it * EB + k, 1), :]).then_inc(e_idx_set, 1)

            def edge_transfers(it, k):
                if not is_first(it):
                    pool.wait_ge(e_h, it * EB + (k - EB + 1))
                if e_inside(it, k + 1):
                    copy_edge_cols(it, k + 1)
                else:
                    pool.wait_ge(e_idx_set, it * EB + k + 1)
                pool.indirect_dma_start(xe[:, k, :], None, x, bass.IndirectOffsetOnAxis(edge_idx[:, k, 0:1], 0),
                                        bounds_check=N - 1, oob_is_err=False).then_inc(e_gathered[k], 16)
                pool.indirect_dma_start(slot_dram, bass.IndirectOffsetOnAxis(edge_idx[:, k, 1:2], 0),
                                        edge_idx[:, k, 2:3], None, bounds_check=N - 1,
                                        oob_is_err=False).then_inc(e_slotted[k], 16)

            pool.wait_ge(slots_cleared, 32)
            copy_edge_cols(0, 0)
            loop(pool, TE, EB, edge_transfers, 1)

            for r in range(EB):
                pool.wait_ge(e_slotted[r], 16 * len(range(r, TE, EB)))
            pool.dma_start(slots[:, 0:TN], slot_dram[0:TN * P, :].rearrange("(p t) a -> p (t a)", t=TN)).then_inc(slots_loaded, 16)
            pool.dma_start(slots[0:NTAIL, TN:NT], slot_dram[TN * P:N, :]).then_inc(slots_loaded, 16)
            pool.wait_ge(slots_loaded, 32)
            for r in range(3):
                pool.wait_ge(e_stored[r], 16 * len(range(r, TE, 3)))

            def copy_slots(it, k):
                if not n_inside(it, k):
                    return
                it, k = later((it, k), NB, 0)
                g = (k // U) % 3
                if n_rows(it, k) < P:
                    nc.gpsimd.tensor_copy(node_idx[0:NTAIL, g, 0:1], slots[0:NTAIL, TN:NT]).then_inc(n_idx_set, 1)
                else:
                    nc.gpsimd.tensor_copy(node_idx[:, g, :], slots[:, bass.ds(it * NB + k, U)]).then_inc(n_idx_set, 1)

            def gather_waits(it, k):
                if not n_inside(it, k):
                    return
                early = is_first(it) and k < 6
                it, k = later((it, k), NB, 0)
                pool.wait_ge(n_idx_set, it * XR + k // U + 1)
                if not early:
                    pool.wait_ge(n_y, it * NB + (k - 6 + 1))

            def gather_nodes(it, k):
                if not n_inside(it, k):
                    return
                it, k = later((it, k), NB, 0)
                rows, r = n_rows(it, k), k % 6
                pool.indirect_dma_start(gathered[0:rows, r, :], None, a_dram,
                                        bass.IndirectOffsetOnAxis(node_idx[0:rows, (k // U) % 3, k % U:k % U + 1], 0),
                                        bounds_check=EP - 1, oob_is_err=False).then_inc(n_gathered[r], 16)

            def add_x(it, k):
                it, k = later((it, k), NB, 0)
                rows = n_rows(it, k)
                pool.wait_ge(n_relu, it * NB + k + 1)
                place = xn[0:rows, k // U, k % U, :]
                nc.gpsimd.tensor_tensor(place, place, y[0:rows, k % 3, :], ALU.add).then_inc(n_added, 1)

            pool.wait_ge(e_h, TE)
            copy_slots(0, 0)
            for k in range(3):
                gather_waits(0, k)
                gather_nodes(0, k)

            def node_step(it, k):
                if k % U == 0:
                    copy_slots(it, k + U)
                gather_waits(it, k + 3)
                if not (is_first(it) and k == 0):
                    add_x(it, k - 1)
                gather_nodes(it, k + 3)

            loop(pool, NT, NB, node_step, 2 * U + 2)
            add_x(NLAST, NT - 1 - NLAST * NB)

        @block.scalar
        def _(act):
            for c in range(KW):
                act.wait_ge(w_turned, c + 1)
                nc.scalar.activation(w_hi[:, c, :], ps_w[c % 4][:, :], ACT.Copy).then_inc(w_hi_set, 1)
            act.wait_ge(consts_set, 4)

            def n_sqrt(it, g):
                if isinstance(it, int) and it * NB + g * U >= NT:
                    return
                it, g = later((it, g), XR, 0)
                rows = n_rows(it, g * U)
                u = U if rows == P else 1
                act.wait_ge(n_aggr, (it * XR + g) + 1)
                nc.scalar.activation(n_small[0:rows, g % 3, 0, 0:u], n_mv[0:rows, g % 3, 0:u, 1], ACT.Sqrt,
                                     bias=eps[0:rows, 0:1]).then_inc(n_sd, 1)

            def n_norm(it, k):
                if not n_inside(it, k):
                    return
                it, k = later((it, k), NB, 0)
                rows, g = n_rows(it, k), k // U
                act.wait_ge(n_chain, (it * XR + g + 1) * CHAIN)
                nc.scalar.activation(hn[0:rows, k % 3, :], xn[0:rows, g, k % U, :], ACT.Relu,
                                     bias=n_small[0:rows, g % 3, 5, k % U:k % U + 1],
                                     scale=n_small[0:rows, g % 3, 4, k % U:k % U + 1]).then_inc(n_h, 1)

            n_sqrt(0, 0)
            n_sqrt(0, 1)
            n_norm(0, 0)
            n_norm(0, 1)

            def e_sqrt(it, q):
                if isinstance(it, int) and it * EB + q * 2 >= TE:
                    return
                it, q = later((it, q), EB // 2, 0)
                act.wait_ge(e_aggr, it * (EB // 2) + q + 1)
                nc.scalar.activation(e_small[:, q, 0, :], e_mv[:, q, :, 1], ACT.Sqrt,
                                     bias=eps[:, 0:1]).then_inc(e_sd, 1)

            def e_norm(it, k):
                if not e_inside(it, k):
                    return
                it, k = later((it, k), EB, 0)
                q = k // 2
                act.wait_ge(e_chain, (it * (EB // 2) + q + 1) * CHAIN)
                nc.scalar.activation(he[:, k % 3, :], xe[:, k, :], ACT.Relu,
                                     bias=e_small[:, q, 5, k % 2:k % 2 + 1],
                                     scale=e_small[:, q, 4, k % 2:k % 2 + 1]).then_inc(e_h, 1)

            def e_high(it, k):
                if not e_inside(it, k):
                    return
                early = is_first(it) and k < 3
                it, k = later((it, k), EB, 0)
                act.wait_ge(e_agg, it * EB + k + 1)
                if not early:
                    act.wait_ge(e_product, it * EB + (k - 3 + 1))
                nc.scalar.activation(agg_hi[:, k % 3, :, :], agg[:, k % 3, :, :], ACT.Copy).then_inc(e_hi, 1)

            def e_scale(it, k):
                early = is_first(it) and k < 3
                it, k = later((it, k), EB, 0)
                act.wait_ge(e_product, it * EB + k + 1)
                if not early:
                    pit, pk = later((it, k), EB, -3)
                    act.wait_ge(e_stored[k % 3], (it * 2 + k // 3) * 16)
                nc.scalar.activation(a_out[:, k % 3, :], ps_a[k % 2][:, :], ACT.Copy,
                                     scale=rdeg_col[:, bass.ds(it * EB + k, 1)]).then_inc(e_out, 1)

            e_sqrt(0, 0)
            e_sqrt(0, 1)
            e_sqrt(0, 2)
            for k in range(3):
                e_norm(0, k)
            for k in range(2):
                e_high(0, k)

            def edge_step(it, k):
                e_high(it, k + 2)
                e_norm(it, k + 3)
                if not (is_first(it) and k == 0):
                    e_scale(it, k - 1)
                if k % 2 == 1:
                    e_sqrt(it, (k + 5) // 2)

            loop(act, TE, EB, edge_step, EB + 1)
            e_scale(ELAST, TE - 1 - ELAST * EB)

            def n_high(it, k):
                if not n_inside(it, k):
                    return
                early = is_first(it) and k < 3
                it, k = later((it, k), NB, 0)
                rows = n_rows(it, k)
                act.wait_ge(n_turned, it * NB + k + 1)
                if early:
                    act.wait_ge(e_product, max(range(k, TE, 3)) + 1)
                else:
                    act.wait_ge(n_product, it * NB + (k - 3 + 1))
                nc.scalar.activation(h_hi[:, k % 3, :, 0:rows],
                                     ps_t[k % 2][:, :].rearrange("p (c n) -> p c n", c=FC)[:, :, 0:rows],
                                     ACT.Copy).then_inc(n_hi, 1)

            def n_relu_step(it, k):
                it, k = later((it, k), NB, 0)
                rows = n_rows(it, k)
                act.wait_ge(n_y, it * NB + k + 1)
                nc.scalar.activation(y[0:rows, k % 3, :], y[0:rows, k % 3, :], ACT.Relu).then_inc(n_relu, 1)

            n_high(0, 0)

            def node_step(it, k):
                n_high(it, k + 1)
                if not (is_first(it) and k == 0):
                    n_relu_step(it, k - 1)
                n_norm(it, k + 2)
                if k % U == U - 1:
                    n_sqrt(it, k // U + 2)

            loop(act, NT, NB, node_step, 2 * U + 2)
            n_relu_step(NLAST, NT - 1 - NLAST * NB)

        @block.vector
        def _(dve):
            step = [0]

            def then(ins):
                step[0] += 1
                ins.then_inc(setup_step, 1)
                dve.wait_ge(setup_step, step[0])

            dve.wait_ge(edges_loaded, 16 * 9)
            then(nc.vector.tensor_tensor(descent[:, :], d_row[:, :], d_next[:, :], ALU.is_gt))
            nc.vector.tensor_reduce(descents[:, :], descent[:, :], axis=AX.X, op=ALU.max).then_inc(descents_set, 1)
            dve.wait_ge(flag_summed, 1)
            nc.vector.tensor_copy(unsorted_flag[:, :], ps_sum[0][0:1, 0:1]).then_inc(flag_set, 1)
            dve.wait_ge(flag_set, 1)

            flag = dve.value_load(unsorted_flag[0:1, 0:1], min_val=0, max_val=EP)
            with dve.If(flag > 0):
                dve.wait_ge(all_loaded, 16)
                dve.wait_ge(sort_loaded, 16 * 4)
                dve.wait_ge(sort_copied, 4)
                nc.vector.tensor_copy(u_dstf[:, :], u_dst[:, :]).then_inc(sort_step, 1)
                dve.wait_ge(sort_step, 1)
                with dve.Fori(0, TE) as j:
                    for c in range(NC):
                        part = d_all[:, c * CH:(c + 1) * CH]
                        nc.vector.tensor_scalar(tied, part, u_dstf[:, bass.ds(j, 1)], 0.0, ALU.is_lt, ALU.add,
                                                accum_out=counts[:, 2 * c:2 * c + 1]).then_inc(sort_step, 1)
                        nc.vector.tensor_scalar(earlier, chunk_pos, float(c * CH),
                                                e_col[:, bass.ds(j, 1)], ALU.add, ALU.is_lt).then_inc(sort_step, 1)
                        dve.wait_ge(sort_step, j * (3 * NC + 1) + (3 * c + 3))
                        nc.vector.scalar_tensor_tensor(out=tied, in0=part, scalar=u_dstf[:, bass.ds(j, 1)],
                                                       in1=earlier, op0=ALU.is_equal, op1=ALU.mult,
                                                       accum_out=counts[:, 2 * c + 1:2 * c + 2]).then_inc(sort_step, 1)
                        dve.wait_ge(sort_step, j * (3 * NC + 1) + (3 * c + 4))
                    nc.vector.reduce_sum(count[:, :], counts[:, :], axis=AX.X).then_inc(sort_step, 1)
                    dve.wait_ge(sort_step, j * (3 * NC + 1) + (3 * NC + 2))
                    nc.vector.tensor_copy(rank[:, bass.ds(j, 1)], count[:, :]).then_inc(ranks_set, 1)
                    dve.wait_ge(ranks_set, j + 1)

            dve.wait_ge(edges_sorted, 1)
            dve.wait_ge(consts_set, 4)
            then(nc.vector.tensor_tensor(begins[:, :], d_row[:, :], d_prev[:, :], ALU.not_equal))
            then(nc.vector.tensor_tensor(begins[:, :], begins[:, :], e_row[:, :], ALU.mult))
            nc.vector.memset(begin_row[:, 0:1], 0.0).then_inc(runs_set, 1)
            nc.vector.tensor_tensor_scan(run_begin[:, :], begins[:, :], begins[:, :], 0.0, ALU.max, ALU.max).then_inc(runs_set, 1)
            then(nc.vector.tensor_tensor(not_last[:, :], d_row[:, :], d_next[:, :], ALU.is_equal))
            nc.vector.scalar_tensor_tensor(out=scatter_row[:, :], in0=not_last[:, :], scalar=float(NOWHERE),
                                           in1=d_row[:, :], op0=ALU.mult, op1=ALU.add).then_inc(rows_set, 1)
            nc.vector.tensor_copy(sf_row[:, :], s_row[:, :]).then_inc(rows_set, 1)
            nc.vector.tensor_copy(df_row[:, :], d_row[:, :]).then_inc(rows_set, 1)
            dve.wait_ge(ends_turned, 1)
            dve.wait_ge(runs_set, 2)
            nc.vector.tensor_copy(begins[0:1, 0:TE], ps_sum[1][0:1, 0:TE]).then_inc(runs_set, 1)
            dve.wait_ge(runs_set, 3)
            nc.vector.tensor_tensor_scan(begin_row[:, 1:TE + 1], begins[0:1, 0:TE], begins[0:1, 0:TE], 0.0,
                                         ALU.max, ALU.max).then_inc(carry_row_set, 1)
            dve.wait_ge(carry_turned, 1)
            dve.wait_ge(runs_set, 3)
            then(nc.vector.tensor_scalar(run_begin[:, :], run_begin[:, :], ps_sum[1][0:TE, 256:257], None, ALU.max))
            then(nc.vector.tensor_tensor(run_begin[:, :], e_row[:, :], run_begin[:, :], ALU.subtract))
            then(nc.vector.tensor_scalar(run_begin[:, :], run_begin[:, :], 1.0, None, ALU.add))
            nc.vector.reciprocal(rdeg_row[:, :], run_begin[:, :]).then_inc(rows_set, 1)
            dve.wait_ge(rows_turned, 1)
            nc.vector.tensor_copy(edge_cols[:, :, 0], ps_a[0][:, 0:TE]).then_inc(cols_set, 1)
            nc.vector.tensor_copy(edge_cols[:, :, 1], ps_a[0][:, TE:2 * TE]).then_inc(cols_set, 1)
            nc.vector.tensor_copy(d_col[:, :], ps_a[0][:, 2 * TE:3 * TE]).then_inc(cols_set, 1)
            nc.vector.tensor_copy(rdeg_col[:, :], ps_a[0][:, 3 * TE:4 * TE]).then_inc(cols_set, 1)
            for c in range(KW):
                dve.wait_ge(w_hi_set, c + 1)
                nc.vector.tensor_tensor(w_lo[:, c, :], ps_w[c % 4][:, :], w_hi[:, c, :].bitcast(F32),
                                        ALU.subtract).then_inc(w_lo_set, 1)

            def chain(small, mv, count_sem, base, rows=slice(0, P)):
                sd, r0, vr, q, r, shift = (small[:, n, :] for n in range(6))
                mean, var = mv[:, :, 0], mv[:, :, 1]
                nc.vector.reciprocal(r0, sd).then_inc(count_sem, 1)
                dve.wait_ge(count_sem, base + 1)
                nc.vector.scalar_tensor_tensor(out=vr, in0=var, scalar=EPS, in1=r0, op0=ALU.add,
                                               op1=ALU.mult).then_inc(count_sem, 1)
                dve.wait_ge(count_sem, base + 2)
                nc.vector.tensor_tensor(q, vr, r0, ALU.mult).then_inc(count_sem, 1)
                dve.wait_ge(count_sem, base + 3)
                nc.vector.tensor_scalar(vr, q, -0.5, 1.5, ALU.mult, ALU.add).then_inc(count_sem, 1)
                dve.wait_ge(count_sem, base + 4)
                nc.vector.tensor_tensor(r, vr, r0, ALU.mult).then_inc(count_sem, 1)
                dve.wait_ge(count_sem, base + 5)
                nc.vector.scalar_tensor_tensor(out=shift, in0=mean, scalar=-1.0, in1=r, op0=ALU.mult,
                                               op1=ALU.mult).then_inc(count_sem, 1)

            def n_stats_step(it, k):
                if not n_inside(it, k):
                    return
                it, k = later((it, k), NB, 0)
                rows, g, u = n_rows(it, k), k // U, k % U
                if u == 0:
                    dve.wait_ge(n_loaded[g], it * 16 + 16)
                nc.vector.bn_stats(n_bn[0:rows, g % 3, u, :], xn[0:rows, g, u, :]).then_inc(n_stats, 1)

            def n_aggr_step(it, g):
                if isinstance(it, int) and it * NB + g * U >= NT:
                    return
                it, g = later((it, g), XR, 0)
                rows = n_rows(it, g * U)
                for v in range(U if rows == P else 1):
                    last = nc.vector.bn_aggr(n_mv[0:rows, g % 3, v, :], n_bn[0:rows, g % 3, v, :])
                last.then_inc(n_aggr, 1)

            def n_chain_step(it, g):
                if isinstance(it, int) and it * NB + g * U >= NT:
                    return
                it, g = later((it, g), XR, 0)
                rows = n_rows(it, g * U)
                u = U if rows == P else 1
                dve.wait_ge(n_sd, (it * XR + g) + 1)
                chain(n_small[0:rows, g % 3, :, 0:u], n_mv[0:rows, g % 3, 0:u, :], n_chain,
                      (it * XR + g) * CHAIN)

            for k in range(2 * U + 1):
                n_stats_step(0, k)
            dve.wait_ge(n_stats, 2 * U)
            for g in range(2):
                n_aggr_step(0, g)
            n_chain_step(0, 0)

            def e_stats_step(it, k):
                if not e_inside(it, k):
                    return
                it, k = later((it, k), EB, 0)
                q = k // 2
                dve.wait_ge(e_gathered[k], it * 16 + 16)
                nc.vector.bn_stats(e_bn[:, q, k % 2, :], xe[:, k, :]).then_inc(e_stats, 1)

            def e_aggr_step(it, q):
                if isinstance(it, int) and it * EB + q * 2 >= TE:
                    return
                it, q = later((it, q), EB // 2, 0)
                for v in range(2):
                    last = nc.vector.bn_aggr(e_mv[:, q, v, :], e_bn[:, q, v, :])
                last.then_inc(e_aggr, 1)

            def e_chain_step(it, q):
                if isinstance(it, int) and it * EB + q * 2 >= TE:
                    return
                it, q = later((it, q), EB // 2, 0)
                dve.wait_ge(e_sd, it * (EB // 2) + q + 1)
                chain(e_small[:, q, :, :], e_mv[:, q, :, :], e_chain, (it * (EB // 2) + q) * CHAIN)

            def e_masks(it, k):
                if not e_inside(it, k):
                    return
                first = is_first(it) and k == 0
                it, k = later((it, k), EB, 0)
                j = it * EB + k
                tile = d_all[:, bass.ds(j * P, P)]
                last = nc.vector.tensor_scalar(same[:, k % 2, :], tile, d_col[:, bass.ds(j, 1)], None, ALU.is_equal)
                if not first:
                    last = nc.vector.tensor_scalar(goes_on[:, k % 2, :], tile, d_all[:, bass.ds(j * P - 1, 1)],
                                                   None, ALU.is_equal)
                last.then_inc(e_same, 1)

            def e_carry(it, k):
                if not e_inside(it, k):
                    return
                first = is_first(it) and k == 0
                it, k = later((it, k), EB, 0)
                dve.wait_ge(e_summed, it * EB + k + 1)
                if first:
                    nc.vector.tensor_copy(agg[:, 0, :, :].rearrange("p c n -> p (c n)"), ps_sum[0][:, :]).then_inc(e_agg, 1)
                    return
                if k % 2 == 1:
                    ahead = k + 5
                    if isinstance(it, int):
                        ahead = min(ahead, TE - it * EB)
                    dve.wait_ge(e_stats, it * EB + ahead)
                dve.wait_ge(e_same, it * EB + k + 1)
                dve.wait_ge(e_agg, it * EB + k)
                for c in range(FC):
                    last = nc.vector.scalar_tensor_tensor(
                        out=agg[:, k % 3, c, :], in0=goes_on[:, k % 2, :], scalar=agg[:, (k - 1) % 3, c, P - 1:P],
                        in1=ps_sum[k % 2][:, c * P:(c + 1) * P], op0=ALU.mult, op1=ALU.add)
                last.then_inc(e_agg, 1)

            def e_low(it, k):
                if not e_inside(it, k):
                    return
                it, k = later((it, k), EB, 0)
                dve.wait_ge(e_hi, it * EB + k + 1)
                nc.vector.tensor_tensor(agg_lo[:, k % 3, :, :], agg[:, k % 3, :, :],
                                        agg_hi[:, k % 3, :, :].bitcast(F32), ALU.subtract).then_inc(e_lo, 1)

            dve.wait_ge(all_loaded, 16)
            dve.wait_ge(cols_set, 4)
            for k in range(EB):
                e_stats_step(0, k)
            dve.wait_ge(e_stats, EB)
            for q in range(3):
                e_aggr_step(0, q)
            e_chain_step(0, 0)
            e_chain_step(0, 1)
            for k in range(2):
                e_masks(0, k)
            for k in range(2):
                e_carry(0, k)
                e_low(0, k)
            e_masks(0, 2)
            e_stats_step(0, EB)

            def edge_step(it, k):
                e_carry(it, k + 2)
                if k % 2 == 1:
                    e_aggr_step(it, (k + 5) // 2)
                else:
                    e_chain_step(it, (k + 4) // 2)
                e_masks(it, k + 3)
                e_low(it, k + 2)
                e_stats_step(it, k + EB + 1)

            loop(dve, TE, EB, edge_step, EB + 1)

            dve.wait_ge(slots_loaded, 32)
            nc.vector.tensor_scalar(has_edges[:, 0:TN], slots[:, 0:TN], float(NOWHERE), None, ALU.is_lt).then_inc(mask_set, 1)
            nc.vector.tensor_scalar(has_edges[0:NTAIL, TN:NT], slots[0:NTAIL, TN:NT], float(NOWHERE), None,
                                    ALU.is_lt).then_inc(mask_set, 1)

            def n_low(it, k):
                if not n_inside(it, k):
                    return
                it, k = later((it, k), NB, 0)
                rows = n_rows(it, k)
                dve.wait_ge(n_hi, it * NB + k + 1)
                nc.vector.tensor_tensor(h_lo[:, k % 3, :, 0:rows],
                                        ps_t[k % 2][:, :].rearrange("p (c n) -> p c n", c=FC)[:, :, 0:rows],
                                        h_hi[:, k % 3, :, 0:rows].bitcast(F32), ALU.subtract).then_inc(n_lo, 1)

            def n_edge_part(it, k):
                early = is_first(it) and k < 3
                it, k = later((it, k), NB, 0)
                if k % U == U - 2:
                    ahead = k + 2 + 2 * U
                    if isinstance(it, int):
                        ahead = min(ahead, NT - it * NB)
                    dve.wait_ge(n_stats, it * NB + ahead)
                rows = n_rows(it, k)
                dve.wait_ge(n_product, it * NB + k + 1)
                dve.wait_ge(n_gathered[k % 6], (it * 3 + k // 6) * 16 + 16)
                if early:
                    dve.wait_ge(e_stored[k], 16 * len(range(k, TE, 3)))
                else:
                    dve.wait_ge(n_added, it * NB + (k - 3 + 1))
                nc.vector.scalar_tensor_tensor(out=y[0:rows, k % 3, :], in0=gathered[0:rows, k % 6, :],
                                               scalar=has_edges[0:rows, bass.ds(it * NB + k, 1)],
                                               in1=ps_y[k % 2][0:rows, :], op0=ALU.mult, op1=ALU.add).then_inc(n_y, 1)

            n_low(0, 0)
            dve.wait_ge(mask_set, 2)

            def node_step(it, k):
                if not (is_first(it) and k == 0):
                    n_edge_part(it, k - 1)
                if k % U == U - 1:
                    n_aggr_step(it, k // U + 2)
                n_low(it, k + 1)
                if k % U == 0:
                    n_chain_step(it, k // U + 1)
                n_stats_step(it, k + 2 * U + 1)

            loop(dve, NT, NB, node_step, 2 * U + 2)
            n_edge_part(NLAST, NT - 1 - NLAST * NB)

        @block.tensor
        def _(pe):
            pe.wait_ge(ident_set, 1)
            pe.wait_ge(consts_set, 1)
            pe.wait_ge(descents_set, 1)
            nc.tensor.matmul(ps_sum[0][0:1, 0:1], ones[0:TE, 0:1], descents[:, :], start=True, stop=True).then_inc(flag_summed, 1)
            pe.wait_ge(w_loaded, 16)

            def turn_w(c):
                if c >= 4:
                    pe.wait_ge(w_lo_set, c - 3)
                for b in range(OC):
                    last = nc.tensor.transpose(ps_w[c % 4][:, b * P:(b + 1) * P], w_rows[:, b, c * P:(c + 1) * P], ident[:, :])
                last.then_inc(w_turned, 1)

            for c in range(4):
                turn_w(c)
            pe.wait_ge(runs_set, 2)
            nc.tensor.matmul(ps_sum[1][0:1, 0:TE], run_begin[:, P - 1:P], ident[0:TE, 0:TE], start=True, stop=True).then_inc(ends_turned, 1)
            pe.wait_ge(carry_row_set, 1)
            nc.tensor.matmul(ps_sum[1][0:TE, 256:257], begin_row[0:1, 0:TE], ones[0:1, 0:1], start=True, stop=True).then_inc(carry_turned, 1)
            pe.wait_ge(rows_set, 4)
            for n, row in enumerate((sf_row, scatter_row, df_row, rdeg_row)):
                last = nc.tensor.transpose(ps_a[0][:, n * TE:(n + 1) * TE], row[:, :], ident[0:TE, 0:TE])
            last.then_inc(rows_turned, 1)
            for c in range(4, KW):
                turn_w(c)
            pe.wait_ge(w_lo_set, KW)
            pe.wait_ge(cols_set, 4)

            def product(ps, hi, lo, w0, rows):
                for c in range(FC):
                    nc.tensor.matmul(ps[0:rows, :], hi[:, c, 0:rows], w_hi[:, w0 + c, :], start=(c == 0), stop=False)
                    nc.tensor.matmul(ps[0:rows, :], hi[:, c, 0:rows], w_lo[:, w0 + c, :], start=False, stop=False)
                for c in range(FC):
                    last = nc.tensor.matmul(ps[0:rows, :], lo[:, c, 0:rows], w_hi[:, w0 + c, :], start=False, stop=(c == FC - 1))
                return last

            def e_sum(it, k):
                if not e_inside(it, k):
                    return
                early = is_first(it) and k < 2
                it, k = later((it, k), EB, 0)
                pe.wait_ge(e_h, it * EB + k + 1)
                pe.wait_ge(e_same, it * EB + k + 1)
                if not early:
                    pe.wait_ge(e_agg, it * EB + (k - 2 + 1))
                for c in range(FC):
                    last = nc.tensor.matmul(ps_sum[k % 2][:, c * P:(c + 1) * P], he[:, k % 3, c * P:(c + 1) * P],
                                            same[:, k % 2, :], start=True, stop=True)
                last.then_inc(e_summed, 1)

            e_sum(0, 0)
            e_sum(0, 1)

            def edge_step(it, k):
                e_sum(it, k + 2)
                pe.wait_ge(e_lo, it * EB + k + 1)
                if not (is_first(it) and k < 2):
                    pe.wait_ge(e_out, it * EB + (k - 2 + 1))
                product(ps_a[k % 2], agg_hi[:, k % 3, :, :], agg_lo[:, k % 3, :, :], FC, P).then_inc(e_product, 1)

            loop(pe, TE, EB, edge_step, EB + 1)

            def n_turn(it, k):
                if not n_inside(it, k):
                    return
                early = is_first(it) and k < 2
                it, k = later((it, k), NB, 0)
                rows = n_rows(it, k)
                pe.wait_ge(n_h, it * NB + k + 1)
                if not early:
                    pe.wait_ge(n_lo, it * NB + (k - 2 + 1))
                for c in range(FC):
                    last = nc.tensor.transpose(ps_t[k % 2][:, c * P:c * P + rows], hn[0:rows, k % 3, c * P:(c + 1) * P],
                                               ident[0:rows, 0:rows])
                last.then_inc(n_turned, 1)

            n_turn(0, 0)

            def node_step(it, k):
                n_turn(it, k + 1)
                rows = n_rows(it, k)
                pe.wait_ge(n_lo, it * NB + k + 1)
                if not (is_first(it) and k < 2):
                    pe.wait_ge(n_y, it * NB + (k - 2 + 1))
                product(ps_y[k % 2], h_hi[:, k % 3, :, :], h_lo[:, k % 3, :, :], 0, rows).then_inc(n_product, 1)

            loop(pe, NT, NB, node_step, 2 * U + 2)


def kernel(x, src, dst, L0_gnn_w):
    import numpy as np
    import concourse.bacc as bacc
    from concourse.bass_utils import run_bass_kernel_spmd

    arrays = {"x": np.ascontiguousarray(x), "src": np.ascontiguousarray(src),
              "dst": np.ascontiguousarray(dst), "w": np.ascontiguousarray(L0_gnn_w)}
    nc = bacc.Bacc("TRN2", target_bir_lowering=False, num_devices=1)
    ins = {n: nc.dram_tensor(n, a.shape, mybir.dt.from_np(a.dtype), kind="ExternalInput").ap()
           for n, a in arrays.items()}
    out = nc.dram_tensor("out", arrays["x"].shape, F32, kind="ExternalOutput").ap()
    build(nc, ins["x"], ins["src"], ins["dst"], ins["w"], out)
    r = run_bass_kernel_spmd(nc, [arrays], core_ids=[0])
    return r.results[0]["out"]
```

```python
from contextlib import ExitStack

import concourse.bass as bass
from concourse import mybir

F32 = mybir.dt.float32
F32R = mybir.dt.float32r
I32 = mybir.dt.int32
ALU = mybir.AluOpType
ACT = mybir.ActivationFunctionType
AX = mybir.AxisListType

P = 128
EPS = 1e-5


def build(nc, x, src, dst, w, out):
    N, F = x.shape
    E = src.shape[0]
    O = w.shape[0]
    FC = F // P
    OC = O // P
    KW = 2 * FC

    TN = N // P
    NTAIL = N - TN * P
    U = 3
    XR = 6
    NB = U * XR
    NT = TN + 1
    TE = -(-E // P)
    EFULL = E // P
    ETAIL = E - EFULL * P
    EP = TE * P
    EB = 6
    PAD = 1 << 16
    NOWHERE = 1 << 20
    assert EB + 1 == 2 * U + 1 and TN % U == 0 and E // TE == P - 1 and E % TE and N < PAD and EP < NOWHERE and 0 < NTAIL and 0 < ETAIL

    a_dram = nc.dram_tensor("edge_rows", [EP, O], F32, kind="Internal").ap()
    slot_dram = nc.dram_tensor("slot_of_node", [N, 1], I32, kind="Internal").ap()
    sdst_dram = nc.dram_tensor("sorted_dst", [EP, 1], I32, kind="Internal").ap()
    ssrc_dram = nc.dram_tensor("sorted_src", [EP, 1], I32, kind="Internal").ap()

    x_grid = x[0:TN * P, :].rearrange("(p t) f -> p t f", t=TN)
    out_grid = out[0:TN * P, :].rearrange("(p t) f -> p t f", t=TN)
    a_tiles = a_dram.rearrange("(j p) o -> p j o", p=P)

    ctx = ExitStack()
    with ctx:
        def sb(name, shape, dt=F32):
            return ctx.enter_context(nc.sbuf_tensor(name, shape, dt))

        def pb(name):
            return ctx.enter_context(nc.psum_tensor(name, [P, 512], F32))

        def sem(name):
            return ctx.enter_context(nc.semaphore(name))

        ident = sb("ident", [P, P])
        ones = sb("ones", [P, P])
        eps = sb("eps", [P, 1])
        root_of_eps = sb("root_of_eps", [P, 1])
        w_rows = sb("w_rows", [P, OC, 2 * F])
        w_hi = sb("w_hi", [P, KW, O], F32R)
        w_lo = sb("w_lo", [P, KW, O], F32R)

        d_wide = sb("d_wide", [TE, P + 2], I32)
        d_prev, d_row, d_next = (d_wide[:, n:n + P] for n in range(3))
        s_row = sb("s_row", [TE, P], I32)
        e_row = sb("e_row", [TE, P], I32)
        d_all = sb("d_all", [P, 1 + EP], I32)
        descent = sb("descent", [TE, P])
        descents = sb("descents", [TE, 1])
        unsorted_flag = sb("unsorted_flag", [1, 1], I32)
        begins = sb("begins", [TE, P])
        run_begin = sb("run_begin", [TE, P])
        begin_row = sb("begin_row", [1, TE + 1])
        rdeg_row = sb("rdeg_row", [TE, P])
        not_last = sb("not_last", [TE, P])
        scatter_row = sb("scatter_row", [TE, P])
        sf_row = sb("sf_row", [TE, P])
        rdeg_col = sb("rdeg_col", [P, TE])
        edge_cols = sb("edge_cols", [P, TE, 3], I32)
        none_yet = sb("none_yet", [P, TN + 1], I32)
        slots = sb("slots", [P, NT], I32)
        has_edges = sb("has_edges", [P, NT])

        xe = sb("xe", [P, EB, F])
        edge_idx = sb("edge_idx", [P, EB, 3], I32)
        e_bn = sb("e_bn", [P, 3, 2, 6])
        e_mv = sb("e_mv", [P, 3, 2, 2])
        e_small = sb("e_small", [P, 3, 6, 2])
        he = sb("he", [P, 3, F])
        goes_on = sb("goes_on", [P, 2, P])
        agg = sb("agg", [P, 3, FC, P])
        op_hi = sb("op_hi", [P, 3, FC, P], F32R)
        op_lo = sb("op_lo", [P, 3, FC, P], F32R)
        agg_hi, agg_lo, h_hi, h_lo = op_hi, op_lo, op_hi, op_lo
        a_out = sb("a_out", [P, 3, O])

        xn = sb("xn", [P, XR, U, F])
        n_bn = sb("n_bn", [P, 3, U, 6])
        n_mv = sb("n_mv", [P, 3, U, 2])
        n_small = sb("n_small", [P, 3, 6, U])
        hn = sb("hn", [P, 3, F])
        gathered = xe
        node_idx = sb("node_idx", [P, 3, U], I32)
        y = a_out

        NC = 16
        CH = EP // NC
        xe_flat = xe[:, :, :].rearrange("p k f -> p (k f)")
        chunk_pos, earlier, tied = (xe_flat[:, n * CH:(n + 1) * CH] for n in range(3))
        u_dst = sb("u_dst", [P, TE], I32)
        u_src = sb("u_src", [P, TE], I32)
        u_dstf = sb("u_dstf", [P, TE])
        e_col = sb("e_col", [P, TE])
        counts = sb("counts", [P, 2 * NC])
        count = sb("count", [P, 1])
        rank = sb("rank", [P, TE], I32)
        sort_cols = sb("sort_cols", [P, 4], I32)

        ps_h = [pb("ps_h0"), pb("ps_h1")]
        ps_a = [pb("ps_a0"), pb("ps_a1")]
        ps_t = [pb("ps_t0"), pb("ps_t1")]
        ps_y = [pb("ps_y0"), pb("ps_y1"), *ps_h, *ps_a]
        ps_w = [ps_t[0], ps_t[1], ps_y[0], ps_y[1]]
        w_order = list(range(FC, KW)) + list(range(FC))

        w_loaded = [sem("w1_loaded"), sem("w2_loaded")]
        pads_set = sem("pads_set")
        edges_loaded = sem("edges_loaded")
        list_kept = sem("list_kept")
        first_targets = sem("first_targets")
        targets_loaded = sem("targets_loaded")
        ident_zero = sem("ident_zero")
        ident_set = sem("ident_set")
        consts_set = sem("consts_set")
        eps_set = sem("eps_set")
        w_turned = sem("w_turned")
        w_hi_set = sem("w_hi_set")
        w_lo_set = sem("w_lo_set")
        descents_set = sem("descents_set")
        flag_summed = sem("flag_summed")
        flag_set = sem("flag_set")
        edges_sorted = sem("edges_sorted")
        none_set = sem("none_set")
        slots_cleared = sem("slots_cleared")
        setup_step = sem("setup_step")
        runs_set = sem("runs_set")
        ends_turned = sem("ends_turned")
        carry_row_set = sem("carry_row_set")
        carry_turned = sem("carry_turned")
        rows_set = sem("rows_set")
        rows_turned = sem("rows_turned")
        cols_set = sem("cols_set")
        slots_loaded = sem("slots_loaded")
        mask_set = sem("mask_set")
        sort_loaded = sem("sort_loaded")
        sort_step = sem("sort_step")
        ranks_set = sem("ranks_set")
        sort_copied = sem("sort_copied")
        sort_moved = sem("sort_moved")
        e_idx_set = sem("e_idx_set")
        e_gathered = [sem(f"e_gathered{k}") for k in range(EB)]
        e_slotted = [sem(f"e_slotted{k}") for k in range(EB)]
        e_stats = sem("e_stats")
        e_aggr = sem("e_aggr")
        e_sd = sem("e_sd")
        e_chain = sem("e_chain")
        e_h = sem("e_h")
        e_mask = sem("e_mask")
        e_turned = sem("e_turned")
        e_agg = sem("e_agg")
        e_hi = sem("e_hi")
        e_lo = sem("e_lo")
        e_product = sem("e_product")
        e_out = sem("e_out")
        e_stored = [sem(f"e_stored{k}") for k in range(3)]
        n_loaded = [sem(f"n_loaded{k}") for k in range(XR)]
        n_stored = [sem(f"n_stored{k}") for k in range(XR)]
        n_idx_set = sem("n_idx_set")
        n_gathered = [sem(f"n_gathered{k}") for k in range(6)]
        n_stats = sem("n_stats")
        n_aggr = sem("n_aggr")
        n_sd = sem("n_sd")
        n_chain = sem("n_chain")
        n_h = sem("n_h")
        n_turned = sem("n_turned")
        n_hi = sem("n_hi")
        n_lo = sem("n_lo")
        n_product = sem("n_product")
        n_y = sem("n_y")
        n_relu = sem("n_relu")
        n_added = sem("n_added")

        CHAIN = 6

        def loop(eng, tiles, body, step, ahead=0):
            full = (tiles - ahead) // body
            for k in range(body):
                step(0, k)
            with eng.Fori(1, full) as it:
                for k in range(body):
                    step(it, k)
            for k in range(tiles - full * body):
                step(full + k // body, k % body)

        def later(i, body, by):
            it, k = i
            return it + (k + by) // body, (k + by) % body

        def is_first(it):
            return isinstance(it, int) and it == 0

        NLAST = NT // NB
        ELAST = TE // EB

        def n_inside(it, k):
            return not isinstance(it, int) or it * NB + k < NT

        def e_inside(it, k):
            return not isinstance(it, int) or it * EB + k < TE

        def e_left(it, k):
            return TE - (it * EB + k) if isinstance(it, int) else 0

        def n_place(k):
            return (k + TE) % 3

        def n_rows(it, k):
            return NTAIL if isinstance(it, int) and it * NB + k == TN else P

        def wide_rows(flat, n):
            rest = n - (EFULL * P - 1)
            return [
                (d_wide[1:EFULL, :], bass.AP(tensor=flat.tensor, offset=P - 1, ap=[[P, EFULL - 1], [1, P + 2]])),
                (d_wide[0:1, 1:P + 2], flat[0:P + 1].rearrange("(j i) -> j i", j=1)),
                (d_wide[EFULL:TE, 0:rest], flat[EFULL * P - 1:n].rearrange("(j i) -> j i", j=1)),
            ]

        block = ctx.enter_context(nc.Block())

        @block.sync
        def _(sp):
            sp.wait_ge(pads_set, 2)
            for to, of in wide_rows(dst, E):
                sp.dma_start(to, of).then_inc(edges_loaded, 16)
            sp.dma_start(s_row[0:EFULL, :], src[0:EFULL * P].rearrange("(j i) -> j i", i=P)).then_inc(edges_loaded, 16)
            sp.dma_start(s_row[EFULL:TE, 0:ETAIL], src[EFULL * P:E].rearrange("(j i) -> j i", j=1)).then_inc(edges_loaded, 16)
            sp.dma_start(w_rows[:, :, F:2 * F], w[:, F:2 * F].rearrange("(b p) f -> p b f", p=P)).then_inc(w_loaded[1], 16)
            sp.wait_ge(edges_loaded, 16 * 5)
            sp.dma_start(sdst_dram.rearrange("(j i) a -> j (i a)", i=P), d_row).then_inc(list_kept, 16)

            def load_targets(it, landed):
                a, n = it * (EB * P), EB * P
                if isinstance(it, int):
                    n = min(n, EP - a)
                sp.dma_start(d_all[:, bass.ds(a + 1, n)],
                             sdst_dram[bass.ds(a, n), :].rearrange("e a -> (e a)").partition_broadcast(P)).then_inc(landed, 16)

            sp.wait_ge(edges_sorted, 1)
            sp.wait_ge(list_kept, 16)
            load_targets(0, first_targets)
            sp.wait_ge(e_gathered[EB - 1], 16)
            sp.wait_ge(first_targets, 16)
            load_targets(1, first_targets)
            sp.dma_start(w_rows[:, :, 0:F], w[:, 0:F].rearrange("(b p) f -> p b f", p=P)).then_inc(w_loaded[0], 16)

            def load_group(it, s):
                t0 = it * NB + s * U
                if isinstance(it, int) and t0 >= TN:
                    if t0 == TN:
                        sp.dma_start(xn[0:NTAIL, s, 0, :], x[TN * P:N, :]).then_inc(n_loaded[s], 16)
                    return
                sp.dma_start(xn[:, s, :, :], x_grid[:, bass.ds(t0, U), :]).then_inc(n_loaded[s], 16)

            def store_edges(it, k):
                sp.wait_ge(e_out, it * EB + k + 1)
                sp.dma_start(a_tiles[:, bass.ds(it * EB + k, 1), :],
                             a_out[:, k % 3:k % 3 + 1, :]).then_inc(e_stored[k % 3], 16)
                if k == 1 and (not isinstance(it, int) or (it + 2) * EB < TE):
                    if not is_first(it):
                        sp.wait_ge(targets_loaded, it * 16)
                    load_targets(it + 2, targets_loaded)
                if isinstance(it, int) and BEHIND_LOOP <= it * EB + k < BEHIND_LOOP + XR - 1:
                    load_group(0, it * EB + k - BEHIND_LOOP)

            SP_AHEAD = 2 * EB + 2
            BEHIND_LOOP = (TE - SP_AHEAD) // EB * EB
            loop(sp, TE, EB, store_edges, SP_AHEAD)

            def node_group(it, s):
                b, ks = later((it, s), XR, XR - 1)
                if not (is_first(it) and s == 0):
                    pit, pk = later((it, s), XR, -1)
                    sp.wait_ge(n_stored[pk], 16 * (pit + 1))
                load_group(b, ks)
                t0 = it * NB + s * U
                if isinstance(it, int) and t0 >= TN:
                    sp.wait_ge(n_added, TN + 1)
                    sp.dma_start(out[TN * P:N, :], xn[0:NTAIL, s, 0, :]).then_inc(n_stored[s], 16)
                    return
                sp.wait_ge(n_added, t0 + U)
                sp.dma_start(out_grid[:, bass.ds(t0, U), :], xn[:, s, :, :]).then_inc(n_stored[s], 16)

            groups = TN // U + 1
            loop(sp, groups, XR, node_group, XR)
            for s in range(XR):
                sp.wait_ge(n_stored[s], 16 * len(range(s, groups, XR)))

        @block.gpsimd
        def _(pool):
            nc.gpsimd.memset(d_wide[:, :], PAD).then_inc(pads_set, 1)
            nc.gpsimd.memset(s_row[:, :], 0).then_inc(pads_set, 1)
            nc.gpsimd.memset(d_all[:, 0:1], -1).then_inc(consts_set, 1)
            nc.gpsimd.memset(ident[:, :], 0.0).then_inc(ident_zero, 1)
            nc.gpsimd.memset(ones[:, :], 1.0).then_inc(consts_set, 1)
            pool.wait_ge(ident_zero, 1)
            nc.gpsimd.affine_select(out=ident[:, :], in_=ident[:, :], compare_op=ALU.not_equal, fill=1.0,
                                    base=0, pattern=[[-1, P]], channel_multiplier=1).then_inc(ident_set, 1)
            nc.gpsimd.memset(eps[:, :], EPS).then_inc(eps_set, 1)
            nc.gpsimd.iota(e_row[:, :], pattern=[[1, P]], base=0, channel_multiplier=P).then_inc(consts_set, 1)
            nc.gpsimd.iota(edge_cols[:, :, 2], pattern=[[P, TE]], base=0, channel_multiplier=1).then_inc(consts_set, 1)
            nc.gpsimd.memset(none_yet[:, :], NOWHERE).then_inc(none_set, 1)
            pool.wait_ge(none_set, 1)
            pool.dma_start(slot_dram[0:TN * P, :].rearrange("(p t) a -> p (t a)", t=TN),
                           none_yet[:, 0:TN]).then_inc(slots_cleared, 16)
            pool.dma_start(slot_dram[TN * P:N, :], none_yet[0:NTAIL, 0:1]).then_inc(slots_cleared, 16)

            pool.wait_ge(flag_set, 1)
            pool.wait_ge(edges_loaded, 16 * 5)
            flag = pool.value_load(unsorted_flag[0:1, 0:1], min_val=0, max_val=EP)
            with pool.If(flag > 0):
                pool.wait_ge(list_kept, 16)
                nc.gpsimd.memset(u_dst[:, :], PAD).then_inc(sort_copied, 1)
                nc.gpsimd.memset(u_src[:, :], 0).then_inc(sort_copied, 1)
                pool.wait_ge(sort_copied, 2)
                PF = E // TE
                for to, of in ((u_dst, dst), (u_src, src)):
                    pool.dma_start(to[0:PF, :], of[0:PF * TE].rearrange("(p j) -> p j", j=TE)).then_inc(sort_loaded, 16)
                    pool.dma_start(to[PF:PF + 1, 0:E - PF * TE], of[PF * TE:E].rearrange("(p j) -> p j", p=1)).then_inc(sort_loaded, 16)
                pool.dma_start(d_all[:, 1:1 + EP], sdst_dram.rearrange("e a -> (e a)").partition_broadcast(P)).then_inc(sort_loaded, 16)
                nc.gpsimd.iota(chunk_pos, pattern=[[1, CH]], base=0, channel_multiplier=0,
                               allow_small_or_imprecise_dtypes=True).then_inc(sort_copied, 1)
                nc.gpsimd.iota(e_col[:, :], pattern=[[1, TE]], base=0, channel_multiplier=TE,
                               allow_small_or_imprecise_dtypes=True).then_inc(sort_copied, 1)
                pool.wait_ge(ranks_set, TE)
                pool.wait_ge(sort_loaded, 16 * 5)
                with pool.Fori(0, TE) as j:
                    nc.gpsimd.tensor_copy(sort_cols[:, 0:1], rank[:, bass.ds(j, 1)]).then_inc(sort_copied, 1)
                    nc.gpsimd.tensor_copy(sort_cols[:, 1:2], u_dst[:, bass.ds(j, 1)]).then_inc(sort_copied, 1)
                    nc.gpsimd.tensor_copy(sort_cols[:, 2:3], u_src[:, bass.ds(j, 1)]).then_inc(sort_copied, 1)
                    pool.wait_ge(sort_copied, j * 4 + 7)
                    nc.gpsimd.tensor_tensor(sort_cols[:, 3:4], sort_cols[:, 1:2], sort_cols[:, 2:3],
                                            ALU.add).then_inc(sort_copied, 1)
                    pool.indirect_dma_start(sdst_dram, bass.IndirectOffsetOnAxis(sort_cols[:, 0:1], 0),
                                            sort_cols[:, 1:2], None, bounds_check=EP - 1,
                                            oob_is_err=False).then_inc(sort_moved, 16)
                    pool.indirect_dma_start(ssrc_dram, bass.IndirectOffsetOnAxis(sort_cols[:, 0:1], 0),
                                            sort_cols[:, 2:3], None, bounds_check=EP - 1,
                                            oob_is_err=False).then_inc(sort_moved, 16)
                    pool.wait_ge(sort_copied, j * 4 + 8)
                    pool.wait_ge(sort_moved, j * 32 + 32)
                sd = sdst_dram.rearrange("e a -> (e a)")
                ss = ssrc_dram.rearrange("e a -> (e a)")
                loads = [*wide_rows(sd, EP), (s_row[:, :], ss.rearrange("(j i) -> j i", i=P))]
                for to, of in loads:
                    pool.dma_start(to, of).then_inc(sort_loaded, 16)
                pool.wait_ge(sort_loaded, 16 * (5 + len(loads)))
            nc.gpsimd.memset(sort_cols[:, :], 0).then_inc(edges_sorted, 1)

            pool.wait_ge(cols_set, 2)

            def copy_edge_cols(it, k):
                if not e_inside(it, k) or (is_first(it) and k < EB):
                    return
                it, k = later((it, k), EB, 0)
                pool.wait_ge(e_slotted[k], it * 16)
                pool.wait_ge(e_gathered[k], it * 16)
                pool.wait_ge(e_idx_set, (it - 1) * EB + k + 1)
                nc.gpsimd.tensor_copy(edge_idx[:, k, :].rearrange("p (a c) -> p a c", a=1),
                                      edge_cols[:, bass.ds(it * EB + k, 1), :]).then_inc(e_idx_set, 1)

            def gather_edges(k):
                pool.indirect_dma_start(xe[:, k, :], None, x, bass.IndirectOffsetOnAxis(edge_idx[:, k, 0:1], 0),
                                        bounds_check=N - 1, oob_is_err=False).then_inc(e_gathered[k], 16)

            def scatter_slots(k):
                pool.indirect_dma_start(slot_dram, bass.IndirectOffsetOnAxis(edge_idx[:, k, 1:2], 0),
                                        edge_idx[:, k, 2:3], None, bounds_check=N - 1,
                                        oob_is_err=False).then_inc(e_slotted[k], 16)

            def edge_transfers(it, k):
                if is_first(it):
                    scatter_slots(k)
                    if k == EB - 1:
                        copy_edge_cols(1, 0)
                    return
                pool.wait_ge(e_h, it * EB + (k - EB + 1))
                if e_inside(it, k + 1):
                    copy_edge_cols(it, k + 1)
                else:
                    pool.wait_ge(e_idx_set, (it - 1) * EB + k + 2)
                gather_edges(k)
                scatter_slots(k)

            nc.gpsimd.tensor_copy(edge_idx[:, :, :], edge_cols[:, 0:EB, :]).then_inc(e_idx_set, 1)
            pool.wait_ge(e_idx_set, 1)
            for k in range(EB):
                gather_edges(k)
            pool.wait_ge(slots_cleared, 32)
            loop(pool, TE, EB, edge_transfers, 1)

            for r in range(EB):
                pool.wait_ge(e_slotted[r], 16 * len(range(r, TE, EB)))
            pool.dma_start(slots[:, 0:TN], slot_dram[0:TN * P, :].rearrange("(p t) a -> p (t a)", t=TN)).then_inc(slots_loaded, 16)
            pool.dma_start(slots[0:NTAIL, TN:NT], slot_dram[TN * P:N, :]).then_inc(slots_loaded, 16)
            pool.wait_ge(slots_loaded, 32)
            for r in range(3):
                pool.wait_ge(e_stored[r], 16 * len(range(r, TE, 3)))

            def copy_slots(it, k):
                if not n_inside(it, k):
                    return
                it, k = later((it, k), NB, 0)
                g = (k // U) % 3
                if n_rows(it, k) < P:
                    nc.gpsimd.tensor_copy(node_idx[0:NTAIL, g, 0:1], slots[0:NTAIL, TN:NT]).then_inc(n_idx_set, 1)
                else:
                    nc.gpsimd.tensor_copy(node_idx[:, g, :], slots[:, bass.ds(it * NB + k, U)]).then_inc(n_idx_set, 1)

            def gather_waits(it, k):
                if not n_inside(it, k):
                    return
                early = is_first(it) and k < 6
                it, k = later((it, k), NB, 0)
                pool.wait_ge(n_idx_set, it * XR + k // U + 1)
                if not early:
                    pool.wait_ge(n_y, it * NB + (k - 6 + 1))

            def gather_nodes(it, k):
                if not n_inside(it, k):
                    return
                it, k = later((it, k), NB, 0)
                rows, r = n_rows(it, k), k % 6
                pool.indirect_dma_start(gathered[0:rows, r, :], None, a_dram,
                                        bass.IndirectOffsetOnAxis(node_idx[0:rows, (k // U) % 3, k % U:k % U + 1], 0),
                                        bounds_check=EP - 1, oob_is_err=False).then_inc(n_gathered[r], 16)

            def add_x(it, k):
                it, k = later((it, k), NB, 0)
                rows = n_rows(it, k)
                pool.wait_ge(n_relu, it * NB + k + 1)
                place = xn[0:rows, k // U, k % U, :]
                nc.gpsimd.tensor_tensor(place, place, y[0:rows, n_place(k), :], ALU.add).then_inc(n_added, 1)

            pool.wait_ge(e_h, TE)
            copy_slots(0, 0)
            for k in range(3):
                gather_waits(0, k)
                gather_nodes(0, k)

            def node_step(it, k):
                if k % U == 0:
                    copy_slots(it, k + U)
                gather_waits(it, k + 3)
                if not (is_first(it) and k == 0):
                    add_x(it, k - 1)
                gather_nodes(it, k + 3)

            loop(pool, NT, NB, node_step, 2 * U + 2)
            add_x(NLAST, NT - 1 - NLAST * NB)

        @block.scalar
        def _(act):
            act.wait_ge(eps_set, 1)
            nc.scalar.activation(root_of_eps[:, :], eps[:, :], ACT.Sqrt)

            def w_high(n):
                act.wait_ge(w_turned, n + 1)
                nc.scalar.activation(w_hi[:, w_order[n], :], ps_w[n % 4][:, :], ACT.Copy).then_inc(w_hi_set, 1)

            for n in range(FC):
                w_high(n)

            def n_sqrt(it, g):
                if isinstance(it, int) and it * NB + g * U >= NT:
                    return
                it, g = later((it, g), XR, 0)
                rows = n_rows(it, g * U)
                u = U if rows == P else 1
                act.wait_ge(n_aggr, (it * XR + g) + 1)
                nc.scalar.activation(n_small[0:rows, g % 3, 0, 0:u], n_mv[0:rows, g % 3, 0:u, 1], ACT.Sqrt,
                                     bias=eps[0:rows, 0:1]).then_inc(n_sd, 1)

            def n_norm(it, k):
                if not n_inside(it, k):
                    return
                it, k = later((it, k), NB, 0)
                rows, g = n_rows(it, k), k // U
                act.wait_ge(n_chain, (it * XR + g + 1) * CHAIN)
                nc.scalar.activation(hn[0:rows, k % 3, :], xn[0:rows, g, k % U, :], ACT.Relu,
                                     bias=n_small[0:rows, g % 3, 5, k % U:k % U + 1],
                                     scale=n_small[0:rows, g % 3, 4, k % U:k % U + 1]).then_inc(n_h, 1)

            def n_high(it, k):
                if not n_inside(it, k):
                    return
                early = is_first(it) and k < 3
                it, k = later((it, k), NB, 0)
                rows = n_rows(it, k)
                act.wait_ge(n_turned, it * NB + k + 1)
                if early:
                    act.wait_ge(e_product, TE - 3 + k + 1)
                else:
                    act.wait_ge(n_product, it * NB + (k - 3 + 1))
                nc.scalar.activation(h_hi[:, n_place(k), :, 0:rows],
                                     ps_t[k % 2][:, :].rearrange("p (c n) -> p c n", c=FC)[:, :, 0:rows],
                                     ACT.Copy).then_inc(n_hi, 1)

            def e_sqrt(it, q):
                if isinstance(it, int) and it * EB + q * 2 >= TE:
                    return
                it, q = later((it, q), EB // 2, 0)
                act.wait_ge(e_aggr, it * (EB // 2) + q + 1)
                nc.scalar.activation(e_small[:, q, 0, :], e_mv[:, q, :, 1], ACT.Sqrt,
                                     bias=eps[:, 0:1]).then_inc(e_sd, 1)

            def e_norm(it, k):
                if not e_inside(it, k):
                    return
                early = is_first(it) and k < 3
                it, k = later((it, k), EB, 0)
                q = k // 2
                if not early:
                    act.wait_ge(e_turned, it * EB + (k - 3 + 1))
                act.wait_ge(e_chain, (it * (EB // 2) + q + 1) * CHAIN)
                nc.scalar.activation(he[:, k % 3, :], xe[:, k, :], ACT.Relu,
                                     bias=e_small[:, q, 5, k % 2:k % 2 + 1],
                                     scale=e_small[:, q, 4, k % 2:k % 2 + 1]).then_inc(e_h, 1)

            def e_high(it, k):
                if not e_inside(it, k):
                    return
                early = is_first(it) and k < 3
                it, k = later((it, k), EB, 0)
                act.wait_ge(e_agg, it * EB + k + 1)
                if not early:
                    act.wait_ge(e_product, it * EB + (k - 3 + 1))
                nc.scalar.activation(agg_hi[:, k % 3, :, :], agg[:, k % 3, :, :], ACT.Copy).then_inc(e_hi, 1)

            def e_scale(it, k):
                early = is_first(it) and k < 3
                it, k = later((it, k), EB, 0)
                act.wait_ge(e_product, it * EB + k + 1)
                if is_first(it) and k == 0:
                    act.wait_ge(cols_set, 3)
                if not early:
                    act.wait_ge(e_stored[k % 3], (it * 2 + k // 3) * 16)
                nc.scalar.activation(a_out[:, k % 3, :], ps_a[k % 2][:, :], ACT.Copy,
                                     scale=rdeg_col[:, bass.ds(it * EB + k, 1)]).then_inc(e_out, 1)

            e_sqrt(0, 0)
            for k in range(2):
                e_norm(0, k)
            e_high(0, 0)
            e_sqrt(0, 1)
            e_high(0, 1)
            e_norm(0, 2)
            e_sqrt(0, 2)

            def edge_step(it, k):
                e_norm(it, k + 3)
                if not (is_first(it) and k == 0):
                    e_scale(it, k - 1)
                e_high(it, k + 2)
                if k % 2 == 1:
                    e_sqrt(it, (k + 5) // 2)
                if is_first(it) and 1 <= k <= FC:
                    w_high(FC + k - 1)
                left = e_left(it, k)
                if left == 4:
                    n_sqrt(0, 0)
                elif left == 2:
                    n_norm(0, 0)
                elif left == 1:
                    n_norm(0, 1)
                    n_high(0, 0)
                    n_sqrt(0, 1)

            loop(act, TE, EB, edge_step, EB + 1)
            e_scale(ELAST, TE - 1 - ELAST * EB)

            def n_relu_step(it, k):
                it, k = later((it, k), NB, 0)
                rows = n_rows(it, k)
                act.wait_ge(n_y, it * NB + k + 1)
                nc.scalar.activation(y[0:rows, n_place(k), :], y[0:rows, n_place(k), :], ACT.Relu).then_inc(n_relu, 1)

            def node_step(it, k):
                norm_first = is_first(it) and k < U
                n_high(it, k + 1)
                if norm_first:
                    n_norm(it, k + 2)
                if not (is_first(it) and k == 0):
                    n_relu_step(it, k - 1)
                if not norm_first:
                    n_norm(it, k + 2)
                if k % U == U - 1:
                    n_sqrt(it, k // U + 2)

            loop(act, NT, NB, node_step, 2 * U + 2)
            n_relu_step(NLAST, NT - 1 - NLAST * NB)

        @block.vector
        def _(dve):
            step = [0]

            def then(ins):
                step[0] += 1
                ins.then_inc(setup_step, 1)
                dve.wait_ge(setup_step, step[0])

            dve.wait_ge(edges_loaded, 16 * 5)
            then(nc.vector.tensor_tensor(descent[:, :], d_row, d_next, ALU.is_gt))
            nc.vector.tensor_reduce(descents[:, :], descent[:, :], axis=AX.X, op=ALU.max).then_inc(descents_set, 1)
            dve.wait_ge(flag_summed, 1)
            nc.vector.tensor_copy(unsorted_flag[:, :], ps_h[0][0:1, 0:1]).then_inc(flag_set, 1)
            dve.wait_ge(flag_set, 1)

            flag = dve.value_load(unsorted_flag[0:1, 0:1], min_val=0, max_val=EP)
            with dve.If(flag > 0):
                dve.wait_ge(sort_loaded, 16 * 5)
                dve.wait_ge(sort_copied, 4)
                nc.vector.tensor_copy(u_dstf[:, :], u_dst[:, :]).then_inc(sort_step, 1)
                dve.wait_ge(sort_step, 1)
                with dve.Fori(0, TE) as j:
                    for c in range(NC):
                        part = d_all[:, 1 + c * CH:1 + (c + 1) * CH]
                        nc.vector.tensor_scalar(tied, part, u_dstf[:, bass.ds(j, 1)], 0.0, ALU.is_lt, ALU.add,
                                                accum_out=counts[:, 2 * c:2 * c + 1]).then_inc(sort_step, 1)
                        nc.vector.tensor_scalar(earlier, chunk_pos, float(c * CH),
                                                e_col[:, bass.ds(j, 1)], ALU.add, ALU.is_lt).then_inc(sort_step, 1)
                        dve.wait_ge(sort_step, j * (3 * NC + 1) + (3 * c + 3))
                        nc.vector.scalar_tensor_tensor(out=tied, in0=part, scalar=u_dstf[:, bass.ds(j, 1)],
                                                       in1=earlier, op0=ALU.is_equal, op1=ALU.mult,
                                                       accum_out=counts[:, 2 * c + 1:2 * c + 2]).then_inc(sort_step, 1)
                        dve.wait_ge(sort_step, j * (3 * NC + 1) + (3 * c + 4))
                    nc.vector.reduce_sum(count[:, :], counts[:, :], axis=AX.X).then_inc(sort_step, 1)
                    dve.wait_ge(sort_step, j * (3 * NC + 1) + (3 * NC + 2))
                    nc.vector.tensor_copy(rank[:, bass.ds(j, 1)], count[:, :]).then_inc(ranks_set, 1)
                    dve.wait_ge(ranks_set, j + 1)

            dve.wait_ge(edges_sorted, 1)
            dve.wait_ge(consts_set, 4)
            then(nc.vector.tensor_tensor(not_last[:, :], d_row, d_next, ALU.is_equal))
            nc.vector.scalar_tensor_tensor(out=scatter_row[:, :], in0=not_last[:, :], scalar=float(NOWHERE),
                                           in1=d_row, op0=ALU.mult, op1=ALU.add).then_inc(rows_set, 1)
            nc.vector.tensor_copy(sf_row[:, :], s_row[:, :]).then_inc(rows_set, 1)
            then(nc.vector.tensor_tensor(begins[:, :], d_row, d_prev, ALU.not_equal))
            then(nc.vector.tensor_tensor(begins[:, :], begins[:, :], e_row[:, :], ALU.mult))
            nc.vector.memset(begin_row[:, 0:1], 0.0).then_inc(runs_set, 1)
            nc.vector.tensor_tensor_scan(run_begin[:, :], begins[:, :], begins[:, :], 0.0, ALU.max, ALU.max).then_inc(runs_set, 1)
            dve.wait_ge(rows_turned, 1)
            nc.vector.tensor_copy(edge_cols[:, :, 0], ps_a[0][:, 0:TE]).then_inc(cols_set, 1)
            nc.vector.tensor_copy(edge_cols[:, :, 1], ps_a[0][:, TE:2 * TE]).then_inc(cols_set, 1)

            def w_low(n):
                dve.wait_ge(w_hi_set, n + 1)
                nc.vector.tensor_tensor(w_lo[:, w_order[n], :], ps_w[n % 4][:, :],
                                        w_hi[:, w_order[n], :].bitcast(F32), ALU.subtract).then_inc(w_lo_set, 1)

            def runs_before_rows():
                dve.wait_ge(ends_turned, 1)
                dve.wait_ge(runs_set, 2)
                nc.vector.tensor_copy(begins[0:1, 0:TE], ps_a[1][0:1, 0:TE]).then_inc(runs_set, 1)
                dve.wait_ge(runs_set, 3)
                nc.vector.tensor_tensor_scan(begin_row[:, 1:TE + 1], begins[0:1, 0:TE], begins[0:1, 0:TE], 0.0,
                                             ALU.max, ALU.max).then_inc(carry_row_set, 1)

            def runs_to_counts():
                dve.wait_ge(carry_turned, 1)
                then(nc.vector.tensor_scalar(run_begin[:, :], run_begin[:, :], ps_a[1][0:TE, 256:257], None, ALU.max))
                then(nc.vector.tensor_tensor(run_begin[:, :], e_row[:, :], run_begin[:, :], ALU.subtract))
                then(nc.vector.tensor_scalar(run_begin[:, :], run_begin[:, :], 1.0, None, ALU.add))
                nc.vector.reciprocal(rdeg_row[:, :], run_begin[:, :]).then_inc(rows_set, 1)

            def chain_op(n, small, mv, count_sem, base):
                sd, r0, vr, q, r, shift = (small[:, m, :] for m in range(6))
                mean, var = mv[:, :, 0], mv[:, :, 1]
                if n > 0:
                    dve.wait_ge(count_sem, base + n)
                if n == 0:
                    nc.vector.reciprocal(r0, sd).then_inc(count_sem, 1)
                elif n == 1:
                    nc.vector.scalar_tensor_tensor(out=vr, in0=var, scalar=EPS, in1=r0, op0=ALU.add,
                                                   op1=ALU.mult).then_inc(count_sem, 1)
                elif n == 2:
                    nc.vector.tensor_tensor(q, vr, r0, ALU.mult).then_inc(count_sem, 1)
                elif n == 3:
                    nc.vector.tensor_scalar(vr, q, -0.5, 1.5, ALU.mult, ALU.add).then_inc(count_sem, 1)
                elif n == 4:
                    nc.vector.tensor_tensor(r, vr, r0, ALU.mult).then_inc(count_sem, 1)
                else:
                    nc.vector.scalar_tensor_tensor(out=shift, in0=mean, scalar=-1.0, in1=r, op0=ALU.mult,
                                                   op1=ALU.mult).then_inc(count_sem, 1)

            def n_stats_step(it, k):
                if not n_inside(it, k):
                    return
                it, k = later((it, k), NB, 0)
                rows, g, u = n_rows(it, k), k // U, k % U
                if u == 0:
                    dve.wait_ge(n_loaded[g], it * 16 + 16)
                nc.vector.bn_stats(n_bn[0:rows, g % 3, u, :], xn[0:rows, g, u, :]).then_inc(n_stats, 1)

            def n_aggr_step(it, g):
                if isinstance(it, int) and it * NB + g * U >= NT:
                    return
                it, g = later((it, g), XR, 0)
                rows = n_rows(it, g * U)
                for v in range(U if rows == P else 1):
                    last = nc.vector.bn_aggr(n_mv[0:rows, g % 3, v, :], n_bn[0:rows, g % 3, v, :])
                last.then_inc(n_aggr, 1)

            def n_chain_step(it, g):
                if isinstance(it, int) and it * NB + g * U >= NT:
                    return
                it, g = later((it, g), XR, 0)
                rows = n_rows(it, g * U)
                u = U if rows == P else 1
                dve.wait_ge(n_sd, (it * XR + g) + 1)
                for n in range(CHAIN):
                    chain_op(n, n_small[0:rows, g % 3, :, 0:u], n_mv[0:rows, g % 3, 0:u, :], n_chain,
                             (it * XR + g) * CHAIN)

            def e_stats_step(it, k):
                if not e_inside(it, k):
                    return
                it, k = later((it, k), EB, 0)
                q = k // 2
                dve.wait_ge(e_gathered[k], it * 16 + 16)
                nc.vector.bn_stats(e_bn[:, q, k % 2, :], xe[:, k, :]).then_inc(e_stats, 1)

            def e_aggr_step(it, q):
                if isinstance(it, int) and it * EB + q * 2 >= TE:
                    return
                it, q = later((it, q), EB // 2, 0)
                for v in range(2):
                    last = nc.vector.bn_aggr(e_mv[:, q, v, :], e_bn[:, q, v, :])
                last.then_inc(e_aggr, 1)

            def e_chain_op(n, it, q):
                if isinstance(it, int) and it * EB + q * 2 >= TE:
                    return
                it, q = later((it, q), EB // 2, 0)
                if n == 0:
                    dve.wait_ge(e_sd, it * (EB // 2) + q + 1)
                chain_op(n, e_small[:, q, :, :], e_mv[:, q, :, :], e_chain, (it * (EB // 2) + q) * CHAIN)

            def e_goes_on(it, k):
                if not e_inside(it, k):
                    return
                it, k = later((it, k), EB, 0)
                if k == 0 and isinstance(it, int) and it == 1:
                    dve.wait_ge(first_targets, 32)
                elif k == 0 and not is_first(it):
                    dve.wait_ge(targets_loaded, (it - 1) * 16)
                j = it * EB + k
                nc.vector.tensor_tensor(goes_on[:, k % 2, :], d_all[:, bass.ds(j * P + 1, P)],
                                        d_all[:, bass.ds(j * P, P)], ALU.is_equal).then_inc(e_mask, 1)

            def e_scan_waits(it, k):
                if not e_inside(it, k):
                    return
                first = is_first(it) and k == 0
                it, k = later((it, k), EB, 0)
                if k % 2 == 1:
                    ahead = k + 5
                    if isinstance(it, int):
                        ahead = min(ahead, TE - it * EB)
                    if not (is_first(it) and k == 1):
                        dve.wait_ge(e_stats, it * EB + ahead)
                dve.wait_ge(e_turned, it * EB + k + 1)
                dve.wait_ge(e_mask, it * EB + k + 1)
                if not first:
                    dve.wait_ge(e_agg, it * EB + k)

            def e_scan(it, k, c):
                if not e_inside(it, k):
                    return
                first = is_first(it) and k == 0
                it, k = later((it, k), EB, 0)
                scanned = nc.vector.tensor_tensor_scan(
                    agg[:, k % 3, c, :], goes_on[:, k % 2, :], ps_h[k % 2][:, c * P:(c + 1) * P],
                    0.0 if first else agg[:, (k - 1) % 3, c, P - 1:P], ALU.mult, ALU.add)
                if c == FC - 1:
                    scanned.then_inc(e_agg, 1)

            def e_low(it, k):
                if not e_inside(it, k):
                    return
                it, k = later((it, k), EB, 0)
                dve.wait_ge(e_hi, it * EB + k + 1)
                nc.vector.tensor_tensor(agg_lo[:, k % 3, :, :], agg[:, k % 3, :, :],
                                        agg_hi[:, k % 3, :, :].bitcast(F32), ALU.subtract).then_inc(e_lo, 1)

            runs_before_rows()
            runs_to_counts()
            for n in range(2):
                w_low(n)
            dve.wait_ge(rows_turned, 2)
            nc.vector.tensor_copy(rdeg_col[:, :], ps_a[0][:, 2 * TE:3 * TE]).then_inc(cols_set, 1)
            for k in range(2):
                e_stats_step(0, k)
            dve.wait_ge(e_stats, 2)
            e_aggr_step(0, 0)
            w_low(2)
            for n in range(CHAIN):
                e_chain_op(n, 0, 0)
            dve.wait_ge(first_targets, 16)
            for k in range(2):
                e_goes_on(0, k)
            w_low(3)
            e_stats_step(0, 2)
            e_stats_step(0, 3)
            e_scan_waits(0, 0)
            for c in range(FC):
                e_scan(0, 0, c)
            dve.wait_ge(e_stats, 4)
            e_aggr_step(0, 1)
            e_low(0, 0)
            e_scan_waits(0, 1)
            for c in range(FC):
                e_scan(0, 1, c)
            for n in range(CHAIN):
                e_chain_op(n, 0, 1)
            e_goes_on(0, 2)
            e_low(0, 1)
            for k in range(4, EB):
                e_stats_step(0, k)
            dve.wait_ge(e_stats, EB)
            e_aggr_step(0, 2)
            e_stats_step(0, EB)

            def edge_step(it, k):
                if k % 2 == 1:
                    e_scan_waits(it, k + 2)
                    for c in range(FC):
                        e_scan(it, k + 2, c)
                    e_aggr_step(it, (k + 5) // 2)
                    e_goes_on(it, k + 3)
                else:
                    e_chain_op(0, it, (k + 4) // 2)
                    e_scan_waits(it, k + 2)
                    for c in range(FC):
                        e_scan(it, k + 2, c)
                        e_chain_op(c + 1, it, (k + 4) // 2)
                    e_goes_on(it, k + 3)
                    e_chain_op(CHAIN - 1, it, (k + 4) // 2)
                e_stats_step(it, k + EB + 1)
                if e_left(it, k) == 4:
                    dve.wait_ge(n_stats, U)
                    n_aggr_step(0, 0)
                e_low(it, k + 2)
                if is_first(it) and 1 <= k <= FC:
                    w_low(FC + k - 1)
                left = e_left(it, k)
                if left == 3:
                    n_chain_step(0, 0)
                if 0 < left <= EB + 1:
                    n_stats_step(0, EB + 1 - left)
                if left == 1:
                    dve.wait_ge(n_stats, 2 * U)
                    n_aggr_step(0, 1)

            loop(dve, TE, EB, edge_step, EB + 1)

            def n_low(it, k):
                if not n_inside(it, k):
                    return
                it, k = later((it, k), NB, 0)
                rows = n_rows(it, k)
                dve.wait_ge(n_hi, it * NB + k + 1)
                nc.vector.tensor_tensor(h_lo[:, n_place(k), :, 0:rows],
                                        ps_t[k % 2][:, :].rearrange("p (c n) -> p c n", c=FC)[:, :, 0:rows],
                                        h_hi[:, n_place(k), :, 0:rows].bitcast(F32), ALU.subtract).then_inc(n_lo, 1)

            n_low(0, 0)

            dve.wait_ge(slots_loaded, 32)
            nc.vector.tensor_scalar(has_edges[:, 0:TN], slots[:, 0:TN], float(NOWHERE), None, ALU.is_lt).then_inc(mask_set, 1)
            nc.vector.tensor_scalar(has_edges[0:NTAIL, TN:NT], slots[0:NTAIL, TN:NT], float(NOWHERE), None,
                                    ALU.is_lt).then_inc(mask_set, 1)

            def n_edge_part(it, k):
                early = is_first(it) and k < 3
                it, k = later((it, k), NB, 0)
                if k % U == U - 2:
                    ahead = k + 2 + 2 * U
                    if isinstance(it, int):
                        ahead = min(ahead, NT - it * NB)
                    dve.wait_ge(n_stats, it * NB + ahead)
                rows = n_rows(it, k)
                dve.wait_ge(n_product, it * NB + k + 1)
                dve.wait_ge(n_gathered[k % 6], (it * 3 + k // 6) * 16 + 16)
                if early:
                    dve.wait_ge(e_stored[n_place(k)], 16 * len(range(n_place(k), TE, 3)))
                else:
                    dve.wait_ge(n_added, it * NB + (k - 3 + 1))
                nc.vector.scalar_tensor_tensor(out=y[0:rows, n_place(k), :], in0=gathered[0:rows, k % 6, :],
                                               scalar=has_edges[0:rows, bass.ds(it * NB + k, 1)],
                                               in1=ps_y[k % 6][0:rows, :], op0=ALU.mult, op1=ALU.add).then_inc(n_y, 1)

            dve.wait_ge(mask_set, 2)

            def node_step(it, k):
                low_first = is_first(it) and k < U
                if low_first:
                    n_low(it, k + 1)
                if not (is_first(it) and k == 0):
                    n_edge_part(it, k - 1)
                if k % U == U - 1:
                    n_aggr_step(it, k // U + 2)
                if not low_first:
                    n_low(it, k + 1)
                if k % U == 0:
                    n_chain_step(it, k // U + 1)
                n_stats_step(it, k + 2 * U + 1)

            loop(dve, NT, NB, node_step, 2 * U + 2)
            n_edge_part(NLAST, NT - 1 - NLAST * NB)

        @block.tensor
        def _(pe):
            pe.wait_ge(ident_set, 1)
            pe.wait_ge(consts_set, 1)
            pe.wait_ge(descents_set, 1)
            nc.tensor.matmul(ps_h[0][0:1, 0:1], ones[0:TE, 0:1], descents[:, :], start=True, stop=True).then_inc(flag_summed, 1)

            pe.wait_ge(rows_set, 2)
            for n, row in enumerate((sf_row, scatter_row)):
                last = nc.tensor.transpose(ps_a[0][:, n * TE:(n + 1) * TE], row[:, :], ident[0:TE, 0:TE])
            last.then_inc(rows_turned, 1)

            def turn_w(n):
                c = w_order[n]
                pe.wait_ge(w_loaded[c // FC], 16)
                if n >= 4:
                    pe.wait_ge(w_lo_set, n - 3)
                for b in range(OC):
                    last = nc.tensor.transpose(ps_w[n % 4][:, b * P:(b + 1) * P], w_rows[:, b, c * P:(c + 1) * P], ident[:, :])
                last.then_inc(w_turned, 1)

            pe.wait_ge(runs_set, 2)
            nc.tensor.matmul(ps_a[1][0:1, 0:TE], run_begin[:, P - 1:P], ident[0:TE, 0:TE], start=True, stop=True).then_inc(ends_turned, 1)
            turn_w(0)
            pe.wait_ge(carry_row_set, 1)
            nc.tensor.matmul(ps_a[1][0:TE, 256:257], begin_row[0:1, 0:TE], ones[0:1, 0:1], start=True, stop=True).then_inc(carry_turned, 1)
            for n in range(1, FC):
                turn_w(n)
            pe.wait_ge(rows_set, 3)
            nc.tensor.transpose(ps_a[0][:, 2 * TE:3 * TE], rdeg_row[:, :], ident[0:TE, 0:TE]).then_inc(rows_turned, 1)

            def product(ps, hi, lo, w0, rows):
                for c in range(FC):
                    nc.tensor.matmul(ps[0:rows, :], hi[:, c, 0:rows], w_hi[:, w0 + c, :], start=(c == 0), stop=False)
                    nc.tensor.matmul(ps[0:rows, :], hi[:, c, 0:rows], w_lo[:, w0 + c, :], start=False, stop=False)
                for c in range(FC):
                    last = nc.tensor.matmul(ps[0:rows, :], lo[:, c, 0:rows], w_hi[:, w0 + c, :], start=False, stop=(c == FC - 1))
                return last

            def n_turn(it, k):
                if not n_inside(it, k):
                    return
                early = is_first(it) and k < 2
                it, k = later((it, k), NB, 0)
                rows = n_rows(it, k)
                pe.wait_ge(n_h, it * NB + k + 1)
                if not early:
                    pe.wait_ge(n_lo, it * NB + (k - 2 + 1))
                for c in range(FC):
                    last = nc.tensor.transpose(ps_t[k % 2][:, c * P:c * P + rows], hn[0:rows, k % 3, c * P:(c + 1) * P],
                                               ident[0:rows, 0:rows])
                last.then_inc(n_turned, 1)

            def e_turn(it, k):
                if not e_inside(it, k):
                    return
                early = is_first(it) and k < 2
                it, k = later((it, k), EB, 0)
                pe.wait_ge(e_h, it * EB + k + 1)
                if not early:
                    pe.wait_ge(e_agg, it * EB + (k - 2 + 1))
                for c in range(FC):
                    last = nc.tensor.transpose(ps_h[k % 2][:, c * P:(c + 1) * P], he[:, k % 3, c * P:(c + 1) * P], ident[:, :])
                last.then_inc(e_turned, 1)

            e_turn(0, 0)
            e_turn(0, 1)
            pe.wait_ge(w_lo_set, FC)
            pe.wait_ge(cols_set, 3)

            def edge_step(it, k):
                if not (is_first(it) and k == 0):
                    e_turn(it, k + 2)
                pe.wait_ge(e_lo, it * EB + k + 1)
                if not (is_first(it) and k < 2):
                    pe.wait_ge(e_out, it * EB + (k - 2 + 1))
                if e_left(it, k) == 1:
                    pe.wait_ge(w_lo_set, KW)
                    n_turn(0, 0)
                product(ps_a[k % 2], agg_hi[:, k % 3, :, :], agg_lo[:, k % 3, :, :], FC, P).then_inc(e_product, 1)
                if is_first(it) and k == 0:
                    e_turn(0, 2)
                if is_first(it) and 1 <= k <= FC:
                    turn_w(FC + k - 1)

            loop(pe, TE, EB, edge_step, EB + 1)

            def node_step(it, k):
                n_turn(it, k + 1)
                rows = n_rows(it, k)
                pe.wait_ge(n_lo, it * NB + k + 1)
                if is_first(it) and k == 4:
                    pe.wait_ge(e_out, TE)
                if not (is_first(it) and k < 6):
                    pe.wait_ge(n_y, it * NB + (k - 6 + 1))
                product(ps_y[k % 6], h_hi[:, n_place(k), :, :], h_lo[:, n_place(k), :, :], 0, rows).then_inc(n_product, 1)

            loop(pe, NT, NB, node_step, 2 * U + 2)


def kernel(x, src, dst, L0_gnn_w):
    import numpy as np
    import concourse.bacc as bacc
    from concourse.bass_utils import run_bass_kernel_spmd

    arrays = {"x": np.ascontiguousarray(x), "src": np.ascontiguousarray(src),
              "dst": np.ascontiguousarray(dst), "w": np.ascontiguousarray(L0_gnn_w)}
    nc = bacc.Bacc("TRN2", target_bir_lowering=False, num_devices=1)
    ins = {n: nc.dram_tensor(n, a.shape, mybir.dt.from_np(a.dtype), kind="ExternalInput").ap()
           for n, a in arrays.items()}
    out = nc.dram_tensor("out", arrays["x"].shape, F32, kind="ExternalOutput").ap()
    build(nc, ins["x"], ins["src"], ins["dst"], ins["w"], out)
    r = run_bass_kernel_spmd(nc, [arrays], core_ids=[0])
    return r.results[0]["out"]
```
